# Optimizing a Trainium2 kernel written in Bass

```python
import numpy as np
import jax
import jax.numpy as jnp

def _softmax(x, axis=-1):
    return jax.nn.softmax(x, axis=axis)

def _gelu(x):
    return jax.nn.gelu(x, approximate=True)

def _silu(x):
    return jax.nn.silu(x)

def _sigmoid(x):
    return jax.nn.sigmoid(x)

def _layernorm(x, axis=-1, eps=1e-05):
    m = jnp.mean(x, axis=axis, keepdims=True)
    v = jnp.var(x, axis=axis, keepdims=True)
    return (x - m) / jnp.sqrt(v + eps)

def _scatter_add(tgt, idx, src, axis=0):
    return tgt.at[idx].add(src)

def _segment_sum(src, seg, n):
    return jax.ops.segment_sum(src, seg, n)
kernel_name = 'mk_seq_postln_d1_jaxref_r8_36794d'

def setup_inputs(seed: int=0):
    np.random.seed(seed)
    _w = jnp.asarray

    def _L0_attn_setup():
        import jax, jax.numpy as jnp
        import numpy as np
        N_LAYERS = 4
        D_MODEL = 128
        D_INNER = 256
        D_STATE = 16
        D_CONV = 4
        DT_RANK = 64
        BATCH = 2
        SEQLEN = 64

        def _silu(v):
            return v * jax.nn.sigmoid(v)

        def _causal_conv(u, w, b):
            up = jnp.pad(u, ((0, 0), (D_CONV - 1, 0), (0, 0)))
            k = w.T[:, None, :]
            out = jax.lax.conv_general_dilated(up, k, window_strides=(1,), padding='VALID', dimension_numbers=('NWC', 'WIO', 'NWC'), feature_group_count=D_INNER)
            return out + b

        def _mamba_layer(x, wi, cw, cb, wx, wdt, bdt, Alog, Dp, wo):
            xz = jnp.einsum('bld,ed->ble', x, wi)
            u, z = jnp.split(xz, 2, axis=-1)
            u = _silu(_causal_conv(u, cw, cb))
            x_dbl = jnp.einsum('bld,ed->ble', u, wx)
            dt = x_dbl[..., :DT_RANK]
            Bm = x_dbl[..., DT_RANK:DT_RANK + D_STATE]
            Cm = x_dbl[..., DT_RANK + D_STATE:]
            delta = jax.nn.softplus(jnp.einsum('blr,dr->bld', dt, wdt) + bdt)
            A = -jnp.exp(Alog)
            dA = jnp.exp(jnp.einsum('bld,dn->bldn', delta, A))
            dBu = jnp.einsum('bld,bln->bldn', delta * u, Bm)

            def step(h, inp):
                dA_t, dBu_t, C_t = inp
                h = dA_t * h + dBu_t
                y = jnp.einsum('bdn,bn->bd', h, C_t)
                return (h, y)
            h0 = jnp.zeros((x.shape[0], D_INNER, D_STATE), x.dtype)
            _, ys = jax.lax.scan(step, h0, (dA.transpose(1, 0, 2, 3), dBu.transpose(1, 0, 2, 3), Cm.transpose(1, 0, 2)))
            y = ys.transpose(1, 0, 2) + u * Dp
            y = y * _silu(z)
            return jnp.einsum('bld,ed->ble', y, wo)
        key = jax.random.key(seed)
        ks = jax.random.split(key, 8)
        s = 0.02
        x = jax.random.normal(ks[0], (BATCH, SEQLEN, D_MODEL), jnp.float32)
        in_proj_w = jax.random.normal(ks[1], (N_LAYERS, 2 * D_INNER, D_MODEL), jnp.float32) * s
        conv_w = jax.random.normal(ks[2], (N_LAYERS, D_INNER, D_CONV), jnp.float32) * 0.1
        conv_b = jnp.zeros((N_LAYERS, D_INNER), jnp.float32)
        x_proj_w = jax.random.normal(ks[3], (N_LAYERS, DT_RANK + 2 * D_STATE, D_INNER), jnp.float32) * s
        dt_proj_w = jax.random.normal(ks[4], (N_LAYERS, D_INNER, DT_RANK), jnp.float32) * DT_RANK ** (-0.5)
        dt = jnp.exp(jax.random.uniform(ks[5], (N_LAYERS, D_INNER), jnp.float32) * (np.log(0.1) - np.log(0.001)) + np.log(0.001))
        dt_proj_b = jnp.log(jnp.expm1(dt))
        A_log = jnp.log(jnp.broadcast_to(jnp.arange(1, D_STATE + 1, dtype=jnp.float32), (N_LAYERS, D_INNER, D_STATE)))
        D = jnp.ones((N_LAYERS, D_INNER), jnp.float32)
        out_proj_w = jax.random.normal(ks[6], (N_LAYERS, D_MODEL, D_INNER), jnp.float32) * s
        return dict(x=x, in_proj_w=in_proj_w, conv_w=conv_w, conv_b=conv_b, x_proj_w=x_proj_w, dt_proj_w=dt_proj_w, dt_proj_b=dt_proj_b, A_log=A_log, D=D, out_proj_w=out_proj_w)
    _L0_attn_in = _L0_attn_setup()

    def _L0_ffn_setup():
        import jax, jax.numpy as jnp
        import numpy as np
        B, S, H, FFN, E = (2, 256, 128, 512, 8)
        key = jax.random.key(seed)
        k0, k1, k2, k3 = jax.random.split(key, 4)
        return {'hidden_states': jax.random.normal(k0, (B, S, H), dtype=jnp.float32), 'Wr': jax.random.normal(k1, (H, E), dtype=jnp.float32) * 0.02, 'br': jnp.zeros((E,), dtype=jnp.float32), 'W1': jax.random.normal(k2, (E, H, FFN), dtype=jnp.float32) * 0.02, 'W2': jax.random.normal(k3, (E, FFN, H), dtype=jnp.float32) * 0.02}
    _L0_ffn_in = _L0_ffn_setup()
    _d = {'L0_attn_x': _L0_attn_in['x'], 'L0_attn_in_proj_w': _L0_attn_in['in_proj_w'], 'L0_attn_conv_w': _L0_attn_in['conv_w'], 'L0_attn_conv_b': _L0_attn_in['conv_b'], 'L0_attn_x_proj_w': _L0_attn_in['x_proj_w'], 'L0_attn_dt_proj_w': _L0_attn_in['dt_proj_w'], 'L0_attn_dt_proj_b': _L0_attn_in['dt_proj_b'], 'L0_attn_A_log': _L0_attn_in['A_log'], 'L0_attn_D': _L0_attn_in['D'], 'L0_attn_out_proj_w': _L0_attn_in['out_proj_w'], 'L0_ffn_Wr': _L0_ffn_in['Wr'], 'L0_ffn_br': _L0_ffn_in['br'], 'L0_ffn_W1': _L0_ffn_in['W1'], 'L0_ffn_W2': _L0_ffn_in['W2']}
    _x0 = _d['L0_attn_x']
    _d['L0_attn_x'] = jax.random.normal(jax.random.fold_in(jax.random.key(seed), 1), (32, 256, 128), dtype=_x0.dtype)
    del _x0
    return _d

def reference(L0_attn_x, L0_attn_in_proj_w, L0_attn_conv_w, L0_attn_conv_b, L0_attn_x_proj_w, L0_attn_dt_proj_w, L0_attn_dt_proj_b, L0_attn_A_log, L0_attn_D, L0_attn_out_proj_w, L0_ffn_Wr, L0_ffn_br, L0_ffn_W1, L0_ffn_W2):

    def _L0_attn_ref(x, in_proj_w, conv_w, conv_b, x_proj_w, dt_proj_w, dt_proj_b, A_log, D, out_proj_w):
        import jax, jax.numpy as jnp
        import numpy as np
        N_LAYERS = 4
        D_MODEL = 128
        D_INNER = 256
        D_STATE = 16
        D_CONV = 4
        DT_RANK = 64
        BATCH = 2
        SEQLEN = 64

        def _silu(v):
            return v * jax.nn.sigmoid(v)

        def _causal_conv(u, w, b):
            up = jnp.pad(u, ((0, 0), (D_CONV - 1, 0), (0, 0)))
            k = w.T[:, None, :]
            out = jax.lax.conv_general_dilated(up, k, window_strides=(1,), padding='VALID', dimension_numbers=('NWC', 'WIO', 'NWC'), feature_group_count=D_INNER)
            return out + b

        def _mamba_layer(x, wi, cw, cb, wx, wdt, bdt, Alog, Dp, wo):
            xz = jnp.einsum('bld,ed->ble', x, wi)
            u, z = jnp.split(xz, 2, axis=-1)
            u = _silu(_causal_conv(u, cw, cb))
            x_dbl = jnp.einsum('bld,ed->ble', u, wx)
            dt = x_dbl[..., :DT_RANK]
            Bm = x_dbl[..., DT_RANK:DT_RANK + D_STATE]
            Cm = x_dbl[..., DT_RANK + D_STATE:]
            delta = jax.nn.softplus(jnp.einsum('blr,dr->bld', dt, wdt) + bdt)
            A = -jnp.exp(Alog)
            dA = jnp.exp(jnp.einsum('bld,dn->bldn', delta, A))
            dBu = jnp.einsum('bld,bln->bldn', delta * u, Bm)

            def step(h, inp):
                dA_t, dBu_t, C_t = inp
                h = dA_t * h + dBu_t
                y = jnp.einsum('bdn,bn->bd', h, C_t)
                return (h, y)
            h0 = jnp.zeros((x.shape[0], D_INNER, D_STATE), x.dtype)
            _, ys = jax.lax.scan(step, h0, (dA.transpose(1, 0, 2, 3), dBu.transpose(1, 0, 2, 3), Cm.transpose(1, 0, 2)))
            y = ys.transpose(1, 0, 2) + u * Dp
            y = y * _silu(z)
            return jnp.einsum('bld,ed->ble', y, wo)
        for i in range(N_LAYERS):
            x = _mamba_layer(x, in_proj_w[i], conv_w[i], conv_b[i], x_proj_w[i], dt_proj_w[i], dt_proj_b[i], A_log[i], D[i], out_proj_w[i])
        return x

    def _L0_ffn_ref(hidden_states, Wr, br, W1, W2):
        import jax, jax.numpy as jnp
        import numpy as np
        B, S, H, FFN, E = (2, 256, 128, 512, 8)
        b, s, h = hidden_states.shape
        x = hidden_states.reshape(-1, h)
        route = jax.nn.sigmoid(x @ Wr + br)
        max_prob = jnp.max(route, axis=1, keepdims=True)
        max_ind = jnp.argmax(route, axis=1)
        out = jnp.zeros_like(x)
        n_experts = Wr.shape[1]
        for e in range(n_experts):
            mask = (max_ind == e)[:, None].astype(x.dtype)
            y = jax.nn.gelu(x @ W1[e], approximate=False) @ W2[e]
            out = out + mask * y
        out = out * max_prob
        return out.reshape(b, s, h)
    x = L0_attn_x
    x = _layernorm(x + _L0_attn_ref(x, L0_attn_in_proj_w, L0_attn_conv_w, L0_attn_conv_b, L0_attn_x_proj_w, L0_attn_dt_proj_w, L0_attn_dt_proj_b, L0_attn_A_log, L0_attn_D, L0_attn_out_proj_w), axis=-1)
    x = _layernorm(x + _L0_ffn_ref(x, L0_ffn_Wr, L0_ffn_br, L0_ffn_W1, L0_ffn_W2), axis=-1)
    return x

_drawn_inputs = setup_inputs


def setup_inputs(seed=0):
    import zlib

    import numpy as np

    out = dict(_drawn_inputs(seed))
    spreads = {'L0_attn_conv_b': (0.0, 0.1), 'L0_attn_D': (1.0, 0.2), 'L0_ffn_br': (0.0, 0.273)}
    factors = {}
    for name, (base, spread) in spreads.items():
        noise = np.random.default_rng([zlib.crc32(name.encode()), seed]).standard_normal(out[name].shape)
        drawn = base * np.exp(spread * noise) if base else spread * noise
        out[name] = jnp.asarray(drawn.astype(out[name].dtype))
    for name, factor in factors.items():
        out[name] = (out[name] * factor).astype(out[name].dtype)
    return out
```

```python
from contextlib import ExitStack

import numpy as np

import concourse.bass as bass
from concourse import mybir

ALU = mybir.AluOpType
ACT = mybir.ActivationFunctionType
F32 = mybir.dt.float32
BF16 = mybir.dt.bfloat16
AX_X = mybir.AxisListType.X

P = 128
LAYERS, D_MODEL, D_INNER, D_STATE, D_CONV, DT_RANK = 4, 128, 256, 16, 4, 64
SEQ = 256
T = 512
SPT = T // SEQ
BLK = T // P
HALVES = D_INNER // P
EXPERTS, FFN = 8, 512
FCH = FFN // P
EPS = 1e-5
STEPS_PER_PAIR = 2 * LAYERS
BC = 2 * D_STATE
PARTS = 3
SIGMOID_ONE = float(25 * np.log(2.0))


def layer_stack_moe(nc, x, w_in, w_bc, w_dt, w_delta, w_out, chan, a_log, sel, ident, w_r, b_r, w1, w2, out):
    tiles = x.shape[0] * x.shape[1] // T
    steps = tiles * LAYERS
    x_t = x.rearrange("s (b p) d -> (s b) p d", p=P).rearrange("(t b) p d -> t p b d", b=BLK)
    out_t = out.rearrange("s (b p) d -> (s b) p d", p=P).rearrange("(t b) p d -> t p b d", b=BLK)

    with ExitStack() as ctx:
        def sb(name, shape, dt=F32):
            return ctx.enter_context(nc.sbuf_tensor(name, shape, dt))

        def bank(name):
            return ctx.enter_context(nc.psum_tensor(name, [P, 512], F32))

        def sem(name):
            return ctx.enter_context(nc.semaphore(name))

        w_in_sb = sb("w_in_sb", [P, LAYERS, 2 * D_INNER])
        w_bc_sb = sb("w_bc_sb", [P, LAYERS, HALVES, PARTS * BC])
        w_dt_sb = sb("w_dt_sb", [P, LAYERS, HALVES, DT_RANK])
        w_delta_sb = sb("w_delta_sb", [DT_RANK, LAYERS, D_INNER])
        w_out_sb = sb("w_out_sb", [P, LAYERS, HALVES, D_MODEL])
        chan_sb = sb("chan_sb", [P, LAYERS, HALVES, D_CONV + 3])
        a_sb = sb("a_sb", [P, LAYERS * HALVES * D_STATE])
        a_exp = sb("a_exp", [P, LAYERS * HALVES * D_STATE])
        sel_sb = sb("sel_sb", [PARTS * BC, BC, P], BF16)
        ident_sb = sb("ident_sb", [P, P])
        w_r_sb = sb("w_r_sb", [P, EXPERTS])
        b_r_sb = sb("b_r_sb", [P, EXPERTS])
        w1_sb = sb("w1_sb", [P, EXPERTS, FFN])
        w2_sb = sb("w2_sb", [P, EXPERTS, FCH, D_MODEL])
        residual = sb("residual", [P, tiles * BLK, D_MODEL])

        x_stage = sb("x_stage", [P, 2, BLK, D_MODEL])
        layer_in = sb("layer_in", [P, 2, T])
        conv = sb("conv", [P, HALVES, T])
        u = sb("u", [P, 2, HALVES, T])
        z_gate = sb("z_gate", [P, 2, HALVES, T])
        bc_rest = sb("bc_rest", [PARTS * BC, T])
        bc_mid = sb("bc_mid", [PARTS * BC, T], BF16)
        bc_parts = sb("bc_parts", [PARTS * BC, 2, T], BF16)
        dt_rows = sb("dt_rows", [DT_RANK, T])
        sp_exp = sb("sp_exp", [P, HALVES, T])
        sp_relu = sb("sp_relu", [P, HALVES, T])
        delta = sb("delta", [P, 2, HALVES, T])
        du = sb("du", [P, 2, HALVES, T])
        dbu = sb("dbu", [P, 2, HALVES * T])
        h_state = sb("h_state", [P, 2, HALVES * T])
        c_bcast = sb("c_bcast", [P, 2, T])
        ch = sb("ch", [P, 2, HALVES, T])
        y_skip = sb("y_skip", [P, HALVES, T])
        gated = sb("gated", [P, HALVES, T])
        warm = sb("warm", [P, 1])

        ps_b, ps_c, ps_da0, ps_da1, ps_y0, ps_y1, ps_j0, ps_j1 = [bank(f"ps{i}") for i in range(8)]
        ps_da, ps_y = [ps_da0, ps_da1], [ps_y0, ps_y1]

        x1 = u
        x1_t = layer_in
        hid = sb("hid", [P, 2, FCH, T])
        moe = conv
        ln_stats = sb("ln_stats", [P, 2, BLK, 6])
        ln_mv = sb("ln_mv", [P, 2, BLK, 2])
        ln_rstd = sb("ln_rstd", [P, 2, BLK])
        var_eps = sb("var_eps", [P, 2, BLK])
        minus_half = sb("minus_half", [P, BLK])
        eps = sb("eps", [P, BLK])
        scratch = sb("scratch", [P, 1])
        lg = sb("lg", [P, BLK, EXPERTS])
        lg_max = sb("lg_max", [P, BLK])
        rank = sb("rank", [P, BLK, EXPERTS])
        prio = sb("prio", [P, BLK, EXPERTS])
        mask = sb("mask", [P, 2, BLK, EXPERTS])
        prob_t = sb("prob_t", [P, BLK])
        prob = sb("prob", [P, 2, BLK])

        names = ["w_loaded", "moe_loaded", "x_loaded0", "x_loaded1", "zeroed", "a_neg", "a_ready",
                 "in_mm", "out_mm", "u_mm", "z_mm", "bc_mm", "dt_mm", "delta_mm",
                 "b_ready", "c_ready", "y_mm",
                 "in_ready", "conv_init", "conv_tap", "conv_done",
                 "u_ready", "z_ready", "bc_hi", "bc_rest_s", "bc_mid_s", "bc_midrow", "bc_lo", "dt_ready",
                 "sp_abs", "sp_e", "sp_ln", "delta_ready", "du_ready",
                 "da_ready", "c_copied", "dbu_ready", "scanned", "ch_ready",
                 "y_taken", "gate_ready", "res_init", "res_done",
                 "st", "mv", "rs", "x1_ready", "xt_mm", "xt_ready", "lg_mm", "rt", "pr", "route_ready", "prob_ready", "var_s",
                 "hid_mm", "hid_ready", "ffn_mm", "ffn_taken", "moe_done", "fin", "st2", "mv2", "rs2", "o_ready", "stored0", "stored1"]
        S = {n: sem(n) for n in names}
        (w_loaded, moe_loaded, x_loaded0, x_loaded1, zeroed, a_neg, a_ready,
         in_mm, out_mm, u_mm, z_mm, bc_mm, dt_mm, delta_mm,
         b_ready, c_ready, y_mm,
         in_ready, conv_init, conv_tap, conv_done,
         u_ready, z_ready, bc_hi, bc_rest_s, bc_mid_s, bc_midrow, bc_lo, dt_ready,
         sp_abs, sp_e, sp_ln, delta_ready, du_ready,
         da_ready, c_copied, dbu_ready, scanned, ch_ready,
         y_taken, gate_ready, res_init, res_done,
         st, mv, rs, x1_ready, xt_mm, xt_ready, lg_mm, rt, pr, route_ready, prob_ready, var_s,
         hid_mm, hid_ready, ffn_mm, ffn_taken, moe_done, fin, st2, mv2, rs2, o_ready, stored0, stored1) = [S[n] for n in names]

        x_loaded, stored = [x_loaded0, x_loaded1], [stored0, stored1]
        WEIGHT_DMAS, MOE_DMAS = 10, 3

        def wait(eng, s, count):
            if isinstance(count, int) and count <= 0:
                return
            eng.wait_ge(s, count)

        def run_steps(eng, step):
            for s in range(2):
                step(s, s)
            loops = (steps - STEPS_PER_PAIR) // STEPS_PER_PAIR
            with eng.Fori(0, loops) as j:
                for k in range(2, 2 + STEPS_PER_PAIR):
                    step(j * STEPS_PER_PAIR + k, k % STEPS_PER_PAIR)
            for s in range(steps - 6, steps):
                step(s, s % STEPS_PER_PAIR)

        def tile_of(s, k):
            if isinstance(s, int):
                return (s // STEPS_PER_PAIR) * 2 + k % 2
            return (s - k) // (STEPS_PER_PAIR // 2) + k % 2

        def pair_of(s, k):
            return s // STEPS_PER_PAIR if isinstance(s, int) else (s - k) // STEPS_PER_PAIR

        block = ctx.enter_context(nc.Block())

        @block.sync
        def _(sp):
            for dst, src in ((ident_sb[:, :], ident), (w_in_sb[:, :, :], w_in), (chan_sb[:, :, :, :], chan),
                             (w_bc_sb[:, :, :, :], w_bc), (w_dt_sb[:, :, :, :], w_dt),
                             (w_delta_sb[:, :, :], w_delta), (a_sb[:, :], a_log), (sel_sb[:, :, :], sel),
                             (w_out_sb[:, :, :, :], w_out), (w_r_sb[:, :], w_r)):
                sp.dma_start(dst, src).then_inc(w_loaded, 16)
            for t in range(2):
                sp.dma_start(x_stage[:, t], x_t[t]).then_inc(x_loaded[t], 16)
            sp.dma_start(w1_sb[:, :, :], w1).then_inc(moe_loaded, 16)
            sp.dma_start(w2_sb[:, :, :, :], w2).then_inc(moe_loaded, 16)
            sp.dma_start(b_r_sb[:, :], b_r.rearrange("(a e) -> a e", a=1).to_broadcast([P, EXPERTS])).then_inc(moe_loaded, 16)
            with sp.Fori(1, tiles // 2) as j:
                for half in range(2):
                    copied = sp.snap(j * 2 + (half - 1))
                    sp.wait_ge(w_loaded, 16 * WEIGHT_DMAS)
                    sp.wait_ge(res_init, copied)
                    sp.dma_start(x_stage[:, half], x_t[bass.ds(j * 2 + half, 1)].rearrange("t p b d -> (t p) b d")
                                 ).then_inc(x_loaded[half], 16)
            with sp.Fori(0, tiles // 2) as j:
                for half in range(2):
                    made = sp.snap(j * 2 + (half + 1))
                    sp.wait_ge(w_loaded, 16 * WEIGHT_DMAS)
                    sp.wait_ge(o_ready, made)
                    sp.dma_start(out_t[bass.ds(j * 2 + half, 1)].rearrange("t p b d -> (t p) b d"),
                                 z_gate[:, half, 0, :].rearrange("p (b d) -> p b d", b=BLK)).then_inc(stored[half], 16)
            for half in range(2):
                sp.wait_ge(stored[half], 16 * (tiles // 2))

        @block.tensor
        def _(pe):
            def project_in(p, k):
                wait(pe, sp_abs, 4 * p)
                if k < 2:
                    pe.wait_ge(x_loaded[k % 2], pair_of(p, k) * 16 + 16)
                    for b in range(BLK):
                        last = pe.transpose(ps_j0[:, b * P:(b + 1) * P], x_stage[:, k % 2, b, :], ident_sb[:, :])
                    last.then_inc(in_mm, 1)
                else:
                    pe.wait_ge(gate_ready, p - 1)
                    for h in range(HALVES):
                        last = pe.matmul(ps_j0[:, :], w_out_sb[:, k // 2 - 1, h, :], gated[:, h, :],
                                         start=(h == 0), stop=(h == HALVES - 1))
                    last.then_inc(in_mm, 1)

            def project_out(s):
                pe.wait_ge(gate_ready, s + 1)
                pe.wait_ge(sp_abs, 4 * steps if isinstance(s, int) and s == steps - 1 else 4 * (s + 1) + 2)
                for b in range(BLK):
                    for h in range(HALVES):
                        last = pe.matmul(ps_j1[:, b * P:(b + 1) * P], gated[:, h, b * P:(b + 1) * P],
                                         w_out_sb[:, LAYERS - 1, h, :], start=(h == 0), stop=(h == HALVES - 1))
                last.then_inc(out_mm, 1)

            def half_in(p, k, dst, which, done):
                pe.matmul(dst[:, :], w_in_sb[:, k // 2, which * P:(which + 1) * P], layer_in[:, k % 2, :],
                          start=True, stop=True).then_inc(done, 1)

            def project_u(p, k):
                pe.wait_ge(in_ready, p + 1)
                wait(pe, sp_abs, 4 * p - 2)
                half_in(p, k, ps_j1, 0, u_mm)
                half_in(p, k, ps_j0, 1, u_mm)

            def project_z(p, k):
                pe.wait_ge(conv_done, 2 * p + 1)
                half_in(p, k, ps_j1, 2, z_mm)
                pe.wait_ge(conv_done, 2 * p + 2)
                half_in(p, k, ps_j0, 3, z_mm)

            def project_bc_dt(p, k):
                pe.wait_ge(u_ready, p + 1)
                pe.wait_ge(z_ready, 2 * p + 1)
                for h in range(HALVES):
                    last = pe.matmul(ps_j1[0:PARTS * BC, :], w_bc_sb[:, k // 2, h, :], u[:, k % 2, h, :],
                                     start=(h == 0), stop=(h == HALVES - 1))
                last.then_inc(bc_mm, 1)
                pe.wait_ge(z_ready, 2 * p + 2)
                for h in range(HALVES):
                    last = pe.matmul(ps_j0[0:DT_RANK, :], w_dt_sb[:, k // 2, h, :], u[:, k % 2, h, :],
                                     start=(h == 0), stop=(h == HALVES - 1))
                last.then_inc(dt_mm, 1)

            def project_delta(p, k):
                pe.wait_ge(dt_ready, p + 1)
                pe.wait_ge(bc_rest_s, p + 1)
                pe.matmul(ps_j1[:, :], w_delta_sb[:, k // 2, 0:P], dt_rows[:, :], start=True, stop=True).then_inc(delta_mm, 1)
                pe.matmul(ps_j0[:, :], w_delta_sb[:, k // 2, P:2 * P], dt_rows[:, :], start=True, stop=True).then_inc(delta_mm, 1)

            def broadcast(s, k, n):
                q = s * D_STATE + n
                if n == 0:
                    pe.wait_ge(bc_midrow, s + 1)
                    pe.wait_ge(bc_lo, s + 1)
                wait(pe, dbu_ready, q)
                pe.matmul(ps_b[:, :], sel_sb[:, n, :], bc_parts[:, k % 2, :], start=True, stop=True).then_inc(b_ready, 1)
                wait(pe, c_copied, q)
                pe.matmul(ps_c[:, :], sel_sb[:, D_STATE + n, :], bc_parts[:, k % 2, :], start=True, stop=True).then_inc(c_ready, 1)

            def sum_states(s, n):
                q = s * D_STATE + n
                pe.wait_ge(ch_ready, q + 1)
                if n == 0:
                    wait(pe, y_taken, s)
                for h in range(HALVES):
                    last = pe.matmul(ps_y[h][:, :], ident_sb[:, :], ch[:, q % 2 if isinstance(q, int) else n % 2, h, :],
                                     start=(n == 0), stop=(n == D_STATE - 1))
                last.then_inc(y_mm, 1)

            def step(s, k):
                k1 = (k + 1) % STEPS_PER_PAIR
                last_step = isinstance(s, int) and s == steps - 1
                for n in range(D_STATE):
                    broadcast(s, k, n)
                    if n == 4 and (k - 1) % STEPS_PER_PAIR >= STEPS_PER_PAIR - 2 and not (isinstance(s, int) and s == 0):
                        project_out(s - 1)
                    if not last_step:
                        if n == 4:
                            project_in(s + 1, k1)
                        if n == 5:
                            if (k - 1) % STEPS_PER_PAIR >= STEPS_PER_PAIR - 2 and not (isinstance(s, int) and s == 0):
                                pe.wait_ge(res_done, tile_of(s - 1, (k - 1) % STEPS_PER_PAIR) + 1)
                            project_u(s + 1, k1)
                        if n == 8:
                            project_z(s + 1, k1)
                        if n == 9:
                            project_bc_dt(s + 1, k1)
                        if n == 11:
                            project_delta(s + 1, k1)
                    if n >= 2:
                        sum_states(s, n - 2)
                sum_states(s, D_STATE - 2)
                sum_states(s, D_STATE - 1)

            pe.wait_ge(w_loaded, 16 * WEIGHT_DMAS)
            project_in(0, 0)
            project_u(0, 0)
            project_z(0, 0)
            project_bc_dt(0, 0)
            project_delta(0, 0)
            run_steps(pe, step)
            project_out(steps - 1)

            pe.wait_ge(moe_loaded, 16 * MOE_DMAS)
            pe.wait_ge(res_done, tiles)

            def prepare(t, half):
                pe.wait_ge(x1_ready, t + 1)
                wait(pe, xt_ready, t)
                for b in range(BLK):
                    last = pe.transpose(ps_b[:, b * P:(b + 1) * P], x1[:, half, 0, b * P:(b + 1) * P], ident_sb[:, :])
                last.then_inc(xt_mm, 1)
                pe.wait_ge(xt_ready, t + 1)
                wait(pe, route_ready, t)
                for b in range(BLK):
                    last = pe.matmul(ps_c[:, b * EXPERTS:(b + 1) * EXPERTS], x1_t[:, half, b * P:(b + 1) * P], w_r_sb[:, :],
                                     start=True, stop=True)
                last.then_inc(lg_mm, 1)

            hid_banks = [ps_da0, ps_da1, ps_y0, ps_y1]
            ffn_banks = [ps_j0, ps_j1]

            def up(t, half, e):
                c = t * EXPERTS + e
                for f in range(FCH):
                    wait(pe, hid_ready, (c - 1) * FCH + f + 1)
                    pe.matmul(hid_banks[f][:, :], w1_sb[:, e, f * P:(f + 1) * P], x1_t[:, half, :],
                              start=True, stop=True).then_inc(hid_mm, 1)

            def down(t, e):
                c = t * EXPERTS + e
                pe.wait_ge(hid_ready, (c + 1) * FCH)
                wait(pe, ffn_taken, c - 1)
                for b in range(BLK):
                    for f in range(FCH):
                        last = pe.matmul(ffn_banks[e % 2][:, b * P:(b + 1) * P], hid[:, e % 2, f, b * P:(b + 1) * P],
                                         w2_sb[:, e, f, :], start=(f == 0), stop=(f == FCH - 1))
                last.then_inc(ffn_mm, 1)

            def tile(t, half, ahead):
                up(t, half, 0)
                for e in range(EXPERTS):
                    if e + 1 < EXPERTS:
                        up(t, half, e + 1)
                    if e == 4 and ahead:
                        prepare(t + 1, 1 - half)
                    down(t, e)

            prepare(0, 0)
            tile(0, 0, True)
            tile(1, 1, True)
            with pe.Fori(1, tiles // 2 - 1) as j:
                tile(j * 2, 0, True)
                tile(j * 2 + 1, 1, True)
            tile(tiles - 2, 0, True)
            tile(tiles - 1, 1, False)

        @block.scalar
        def _(act):
            CONV_B, DELTA_B, SKIP = D_CONV, D_CONV + 1, D_CONV + 2

            def chan_of(k, h, c):
                return chan_sb[:, k // 2, h, c:c + 1]

            def take_in(p, k):
                act.wait_ge(in_mm, p + 1)
                act.copy(layer_in[:, k % 2, :], ps_j0[:, :]).then_inc(in_ready, 1)
                if k < 2:
                    act.copy(residual[:, bass.ds(tile_of(p, k) * BLK, BLK), :], x_stage[:, k % 2]
                             ).then_inc(res_init, 1)

            def start_conv(p, k):
                for h, bk in ((0, ps_j1), (1, ps_j0)):
                    act.wait_ge(u_mm, 2 * p + h + 1)
                    act.activation(conv[:, h, :], bk[:, :], ACT.Identity, bias=chan_of(k, h, CONV_B),
                                   scale=chan_of(k, h, D_CONV - 1)).then_inc(conv_init, 1)

            def silus(p, k):
                act.wait_ge(conv_done, 2 * p + 2)
                wait(act, y_taken, p - 1)
                act.activation(u[:, k % 2], conv[:, :, :], ACT.Silu).then_inc(u_ready, 1)
                wait(act, gate_ready, p - 1)
                for h, bk in ((0, ps_j1), (1, ps_j0)):
                    act.wait_ge(z_mm, 2 * p + h + 1)
                    act.activation(z_gate[:, k % 2, h, :], bk[:, :], ACT.Silu).then_inc(z_ready, 1)

            def split_high(p, k):
                act.wait_ge(bc_mm, p + 1)
                act.copy(bc_parts[:, k % 2, :], ps_j1[0:PARTS * BC, :]).then_inc(bc_hi, 1)
                act.wait_ge(dt_mm, p + 1)
                act.copy(dt_rows[:, :], ps_j0[0:DT_RANK, :]).then_inc(dt_ready, 1)

            def split_mid(p, k):
                act.wait_ge(bc_rest_s, p + 1)
                act.copy(bc_mid[:, :], bc_rest[:, :]).then_inc(bc_mid_s, 1)
                act.wait_ge(bc_mid_s, p + 1)
                act.copy(bc_parts[BC:2 * BC, k % 2, :], bc_mid[BC:2 * BC, :]).then_inc(bc_midrow, 1)

            def softplus(p, k):
                wait(act, delta_ready, p)
                for h, bk in ((0, ps_j1), (1, ps_j0)):
                    act.wait_ge(delta_mm, 2 * p + h + 1)
                    act.activation(sp_exp[:, h, :], bk[:, :], ACT.Abs, bias=chan_of(k, h, DELTA_B)).then_inc(sp_abs, 1)
                    act.activation(sp_relu[:, h, :], bk[:, :], ACT.Relu, bias=chan_of(k, h, DELTA_B)).then_inc(sp_abs, 1)
                act.activation(warm[:, :], ident_sb[:, 0:1], ACT.Ln, bias=1.0)
                act.wait_ge(sp_abs, 4 * (p + 1))
                act.activation(sp_exp[:, :, :], sp_exp[:, :, :], ACT.Exp, scale=-1.0).then_inc(sp_e, 1)
                act.wait_ge(sp_e, p + 1)
                act.activation(sp_exp[:, :, :], sp_exp[:, :, :], ACT.Ln, bias=1.0).then_inc(sp_ln, 1)

            def decay(s, k, n):
                q = s * D_STATE + n
                if n == 0:
                    act.wait_ge(delta_ready, s + 1)
                for h in range(HALVES):
                    wait(act, scanned, 2 * q - 1 + h)
                    col = (k // 2 * HALVES + h) * D_STATE + n
                    act.activation(ps_da[h][:, :].rearrange("p (s t) -> p s t", s=SPT)[:, :, 1:SEQ],
                                   delta[:, k % 2, h, :].rearrange("p (s t) -> p s t", s=SPT)[:, :, 1:SEQ],
                                   ACT.Exp, scale=a_sb[:, col:col + 1]).then_inc(da_ready, 1)
                wait(act, ch_ready, q - 1)
                act.wait_ge(c_ready, q + 1)
                act.copy(c_bcast[:, n % 2, :], ps_c[:, :]).then_inc(c_copied, 1)

            def step(s, k):
                k1 = (k + 1) % STEPS_PER_PAIR
                last_step = isinstance(s, int) and s == steps - 1
                for n in range(D_STATE):
                    decay(s, k, n)
                    if not last_step:
                        if n == 4:
                            take_in(s + 1, k1)
                        if n == 5:
                            start_conv(s + 1, k1)
                        if n == 8:
                            silus(s + 1, k1)
                        if n == 9:
                            split_high(s + 1, k1)
                        if n == 10:
                            split_mid(s + 1, k1)
                        if n == 11:
                            softplus(s + 1, k1)

            act.wait_ge(w_loaded, 16 * WEIGHT_DMAS)
            act.activation(a_exp[:, :], a_sb[:, :], ACT.Exp).then_inc(a_neg, 1)
            act.wait_ge(a_neg, 1)
            act.mul(a_sb[:, :], a_exp[:, :], -1.0).then_inc(a_ready, 1)
            take_in(0, 0)
            start_conv(0, 0)
            silus(0, 0)
            split_high(0, 0)
            split_mid(0, 0)
            softplus(0, 0)
            act.wait_ge(a_ready, 1)
            act.wait_ge(zeroed, 2)
            run_steps(act, step)

            hid_banks = [ps_da0, ps_da1, ps_y0, ps_y1]

            def prepare(t, half):
                act.wait_ge(xt_mm, t + 1)
                act.copy(x1_t[:, half, :], ps_b[:, :]).then_inc(xt_ready, 1)
                act.wait_ge(rt, 6 * t + 3)
                act.activation(prob_t[:, :], lg_max[:, :], ACT.Tanh, scale=0.5).then_inc(pr, 1)

            def gelu(t, e):
                c = t * EXPERTS + e
                wait(act, ffn_mm, c - 1)
                for f in range(FCH):
                    act.wait_ge(hid_mm, c * FCH + f + 1)
                    act.activation(hid[:, e % 2, f, :], hid_banks[f][:, :], ACT.Gelu).then_inc(hid_ready, 1)

            def tile(t, half, ahead):
                gelu(t, 0)
                for e in range(EXPERTS):
                    if e + 1 < EXPERTS:
                        gelu(t, e + 1)
                    if e == 4 and ahead:
                        prepare(t + 1, 1 - half)

            prepare(0, 0)
            tile(0, 0, True)
            tile(1, 1, True)
            with act.Fori(1, tiles // 2 - 1) as j:
                tile(j * 2, 0, True)
                tile(j * 2 + 1, 1, True)
            tile(tiles - 2, 0, True)
            tile(tiles - 1, 1, False)

        @block.vector
        def _(dve):
            SKIP = D_CONV + 2

            def conv_taps(p, k, shift, h):
                bk = (ps_j1, ps_j0)[h]
                src = bk[:, :].rearrange("p (s t) -> p s t", s=SPT)[:, :, 0:SEQ - shift]
                acc = conv[:, h, :].rearrange("p (s t) -> p s t", s=SPT)[:, :, shift:SEQ]
                if shift == 1:
                    dve.wait_ge(conv_init, 2 * p + h + 1)
                else:
                    dve.wait_ge(conv_tap, 4 * p + 2 * (shift - 2) + h + 1)
                tap = dve.scalar_tensor_tensor(acc, src, chan_sb[:, k // 2, h, D_CONV - 1 - shift:D_CONV - shift], acc,
                                               ALU.mult, ALU.add)
                if shift < D_CONV - 1:
                    tap.then_inc(conv_tap, 1)
                else:
                    tap.then_inc(conv_done, 1)

            def split_rest(p, k):
                dve.wait_ge(bc_hi, p + 1)
                wait(dve, bc_mid_s, p)
                dve.tensor_tensor(bc_rest[:, :], ps_j1[0:PARTS * BC, :], bc_parts[:, k % 2, :], ALU.subtract
                                  ).then_inc(bc_rest_s, 1)

            def split_low(p, k):
                dve.wait_ge(bc_mid_s, p + 1)
                dve.tensor_tensor(bc_parts[2 * BC:3 * BC, k % 2, :], bc_rest[2 * BC:3 * BC, :], bc_mid[2 * BC:3 * BC, :],
                                  ALU.subtract).then_inc(bc_lo, 1)

            def take_y(s, k):
                dve.wait_ge(y_mm, (s + 1) * D_STATE)
                wait(dve, gate_ready, s)
                for h in range(HALVES):
                    last = dve.scalar_tensor_tensor(y_skip[:, h, :], u[:, k % 2, h, :], chan_sb[:, k // 2, h, SKIP:SKIP + 1],
                                                    ps_y[h][:, :], ALU.mult, ALU.add)
                last.then_inc(y_taken, 1)

            def add_residual(s, k):
                t = tile_of(s, k)
                dve.wait_ge(out_mm, t + 1)
                dve.wait_ge(res_init, t + 1)
                rows = residual[:, bass.ds(t * BLK, BLK), :]
                dve.tensor_tensor(rows, ps_j1[:, :].rearrange("p (b d) -> p b d", b=BLK), rows, ALU.add).then_inc(res_done, 1)

            def inputs(s, k, n):
                q = s * D_STATE + n
                if n == 0:
                    dve.wait_ge(du_ready, s + 1)
                dve.wait_ge(b_ready, q + 1)
                wait(dve, scanned, 2 * (q - 1))
                dve.tensor_tensor(dbu[:, n % 2, :].rearrange("p (h t) -> p h t", h=HALVES), du[:, k % 2],
                                  ps_b[:, :].unsqueeze(1).to_broadcast([P, HALVES, T]), ALU.mult).then_inc(dbu_ready, 1)

            def scan(s, n):
                q = s * D_STATE + n
                dve.wait_ge(dbu_ready, q + 1)
                wait(dve, ch_ready, q - 1)
                for h in range(HALVES):
                    dve.wait_ge(da_ready, 2 * q + h + 1)
                    dve.tensor_tensor_scan(h_state[:, n % 2, h * T:(h + 1) * T], ps_da[h][:, :],
                                           dbu[:, n % 2, h * T:(h + 1) * T], 0.0, ALU.mult, ALU.add).then_inc(scanned, 1)

            def step(s, k):
                k1 = (k + 1) % STEPS_PER_PAIR
                km = (k - 1) % STEPS_PER_PAIR
                first_step = isinstance(s, int) and s == 0
                last_step = isinstance(s, int) and s == steps - 1
                inputs(s, k, 0)
                for n in range(D_STATE):
                    if n + 1 < D_STATE:
                        inputs(s, k, n + 1)
                    scan(s, n)
                    if n == 1 and not first_step:
                        take_y(s - 1, km)
                    if n == 4 and km >= STEPS_PER_PAIR - 2 and not first_step:
                        add_residual(s - 1, km)
                    if not last_step:
                        if n in (5, 6, 7):
                            for h in range(HALVES):
                                conv_taps(s + 1, k1, n - 4, h)
                        if n == 9:
                            split_rest(s + 1, k1)
                        if n == 11:
                            split_low(s + 1, k1)

            dve.memset(ps_da0[:, :], 0.0).then_inc(zeroed, 1)
            dve.memset(ps_da1[:, :], 0.0).then_inc(zeroed, 1)
            dve.wait_ge(w_loaded, 16 * WEIGHT_DMAS)
            for shift in (1, 2, 3):
                for h in range(HALVES):
                    conv_taps(0, 0, shift, h)
            split_rest(0, 0)
            split_low(0, 0)
            run_steps(dve, step)
            take_y(steps - 1, STEPS_PER_PAIR - 1)
            add_residual(steps - 1, STEPS_PER_PAIR - 1)

            ffn_banks = [ps_j0, ps_j1]

            def blocks(ap):
                return ap.rearrange("p (b d) -> p b d", b=BLK)

            def norm_in(t, half):
                for b in range(BLK):
                    last = dve.bn_stats(ln_stats[:, 0, b, :], residual[:, bass.ds(t * BLK + b, 1), :].rearrange("p a d -> p (a d)"))
                last.then_inc(st, 1)
                dve.wait_ge(st, t + 1)
                dve.memset(scratch[:, :], 0.0)
                for b in range(BLK):
                    last = dve.bn_aggr(ln_mv[:, 0, b, :], ln_stats[:, 0, b, :])
                last.then_inc(mv, 1)
                dve.wait_ge(rs, t + 1)
                for b in range(BLK):
                    last = dve.tensor_scalar(x1[:, half, 0, b * P:(b + 1) * P],
                                             residual[:, bass.ds(t * BLK + b, 1), :].rearrange("p a d -> p (a d)"),
                                             ln_mv[:, 0, b, 0:1], ln_rstd[:, 0, b:b + 1], ALU.subtract, ALU.mult)
                last.then_inc(x1_ready, 1)

            def route(t, half):
                dve.wait_ge(lg_mm, t + 1)
                dve.tensor_tensor(lg[:, :, :], ps_c[:, 0:BLK * EXPERTS].rearrange("p (b e) -> p b e", b=BLK),
                                  b_r_sb[:, :].unsqueeze(1).to_broadcast([P, BLK, EXPERTS]), ALU.add).then_inc(rt, 1)
                dve.wait_ge(rt, 6 * t + 1)
                dve.tensor_scalar(lg[:, :, :], lg[:, :, :], SIGMOID_ONE, None, ALU.min).then_inc(rt, 1)
                dve.wait_ge(rt, 6 * t + 2)
                wait(dve, pr, t)
                dve.tensor_reduce(lg_max[:, :], lg[:, :, :], AX_X, ALU.max).then_inc(rt, 1)
                dve.wait_ge(rt, 6 * t + 3)
                dve.tensor_tensor(rank[:, :, :], lg[:, :, :], lg_max[:, :].unsqueeze(2).to_broadcast([P, BLK, EXPERTS]),
                                  ALU.is_equal).then_inc(rt, 1)
                dve.wait_ge(rt, 6 * t + 4)
                dve.tensor_tensor(rank[:, :, :], rank[:, :, :], prio[:, :, :], ALU.mult).then_inc(rt, 1)
                dve.wait_ge(rt, 6 * t + 5)
                dve.tensor_reduce(prob[:, half, :], rank[:, :, :], AX_X, ALU.max).then_inc(rt, 1)
                dve.wait_ge(rt, 6 * t + 6)
                dve.tensor_tensor(mask[:, half], rank[:, :, :], prob[:, half, :].unsqueeze(2).to_broadcast([P, BLK, EXPERTS]),
                                  ALU.is_equal).then_inc(route_ready, 1)
                dve.wait_ge(route_ready, t + 1)
                dve.wait_ge(pr, t + 1)
                dve.tensor_scalar(prob[:, half, :], prob_t[:, :], 0.5, 0.5, ALU.mult, ALU.add).then_inc(prob_ready, 1)

            def combine(t, half, e):
                c = t * EXPERTS + e
                dve.wait_ge(ffn_mm, c + 1)
                wait(dve, ffn_taken, c)
                for b in range(BLK):
                    cols = slice(b * P, (b + 1) * P)
                    m = mask[:, half, b, e:e + 1]
                    if e == 0:
                        last = dve.tensor_scalar(moe[:, 0, cols], ffn_banks[e % 2][:, cols], m, None, ALU.mult)
                    else:
                        last = dve.scalar_tensor_tensor(moe[:, 0, cols], ffn_banks[e % 2][:, cols], m, moe[:, 0, cols],
                                                        ALU.mult, ALU.add)
                last.then_inc(ffn_taken, 1)

            def finish(t, half):
                dve.wait_ge(ffn_taken, (t + 1) * EXPERTS)
                dve.wait_ge(prob_ready, t + 1)
                for b in range(BLK):
                    cols = slice(b * P, (b + 1) * P)
                    last = dve.scalar_tensor_tensor(moe[:, 1, cols], moe[:, 0, cols], prob[:, half, b:b + 1],
                                                    x1[:, half, 0, cols], ALU.mult, ALU.add)
                last.then_inc(fin, 1)
                dve.wait_ge(fin, t + 1)
                for b in range(BLK):
                    last = dve.bn_stats(ln_stats[:, 1, b, :], moe[:, 1, b * P:(b + 1) * P])
                last.then_inc(st2, 1)
                dve.wait_ge(st2, t + 1)
                dve.memset(scratch[:, :], 0.0)
                for b in range(BLK):
                    last = dve.bn_aggr(ln_mv[:, 1, b, :], ln_stats[:, 1, b, :])
                last.then_inc(mv2, 1)
                dve.wait_ge(rs2, t + 1)
                wait(dve, stored[half], 8 * (t - half))
                for b in range(BLK):
                    cols = slice(b * P, (b + 1) * P)
                    last = dve.tensor_scalar(z_gate[:, half, 0, cols], moe[:, 1, cols], ln_mv[:, 1, b, 0:1],
                                             ln_rstd[:, 1, b:b + 1], ALU.subtract, ALU.mult)
                last.then_inc(o_ready, 1)

            def tile(t, half, ahead):
                for e in range(EXPERTS):
                    if e == 2 and ahead:
                        norm_in(t + 1, 1 - half)
                    combine(t, half, e)
                    if e == 5 and ahead:
                        route(t + 1, 1 - half)
                finish(t, half)

            dve.wait_ge(moe_loaded, 16 * MOE_DMAS)
            dve.wait_ge(res_done, tiles)
            for e in range(EXPERTS):
                last = dve.memset(prio[:, :, e:e + 1], float(EXPERTS - e))
            last.then_inc(zeroed, 1)
            dve.wait_ge(zeroed, 3)
            norm_in(0, 0)
            route(0, 0)
            tile(0, 0, True)
            tile(1, 1, True)
            with dve.Fori(1, tiles // 2 - 1) as j:
                tile(j * 2, 0, True)
                tile(j * 2 + 1, 1, True)
            tile(tiles - 2, 0, True)
            tile(tiles - 1, 1, False)

        @block.gpsimd
        def _(pool):
            def make_delta(p, k):
                pool.wait_ge(sp_ln, p + 1)
                pool.tensor_tensor(delta[:, k % 2], sp_relu[:, :, :], sp_exp[:, :, :], ALU.add).then_inc(delta_ready, 1)

            def make_du(p, k):
                pool.wait_ge(delta_ready, p + 1)
                pool.wait_ge(u_ready, p + 1)
                pool.tensor_tensor(du[:, k % 2], delta[:, k % 2], u[:, k % 2], ALU.mult).then_inc(du_ready, 1)

            def gate(s, k):
                pool.wait_ge(y_taken, s + 1)
                pool.wait_ge(z_ready, 2 * (s + 1))
                if (k - 1) % STEPS_PER_PAIR < STEPS_PER_PAIR - 2:
                    wait(pool, in_mm, s + 2 if not (isinstance(s, int) and s == 0) else 0)
                else:
                    wait(pool, out_mm, tile_of(s - 1, (k - 1) % STEPS_PER_PAIR) + 1 if not (isinstance(s, int) and s == 0) else 0)
                pool.tensor_tensor(gated[:, :, :], y_skip[:, :, :], z_gate[:, k % 2], ALU.mult).then_inc(gate_ready, 1)

            def weigh(s, n):
                q = s * D_STATE + n
                pool.wait_ge(scanned, 2 * (q + 1))
                pool.wait_ge(c_copied, q + 1)
                wait(pool, y_mm, q - 1)
                pool.tensor_tensor(ch[:, n % 2], h_state[:, n % 2, :].rearrange("p (h t) -> p h t", h=HALVES),
                                   c_bcast[:, n % 2, :].unsqueeze(1).to_broadcast([P, HALVES, T]), ALU.mult
                                   ).then_inc(ch_ready, 1)

            def step(s, k):
                k1 = (k + 1) % STEPS_PER_PAIR
                for n in range(D_STATE):
                    weigh(s, n)
                    if n == 2 and not (isinstance(s, int) and s == 0):
                        gate(s - 1, (k - 1) % STEPS_PER_PAIR)
                    if not (isinstance(s, int) and s == steps - 1):
                        if n == 12:
                            make_delta(s + 1, k1)
                        if n == 13:
                            make_du(s + 1, k1)

            make_delta(0, 0)
            make_du(0, 0)
            run_steps(pool, step)
            gate(steps - 1, STEPS_PER_PAIR - 1)

            def rstd(which, t, have, done, nth):
                pool.wait_ge(have, t + 1)
                pool.tensor_tensor(var_eps[:, which, :], ln_mv[:, which, :, 1], eps[:, :], ALU.add).then_inc(var_s, 1)
                pool.wait_ge(var_s, nth)
                pool.tensor_tensor(ln_rstd[:, which, :], var_eps[:, which, :], minus_half[:, :], ALU.pow).then_inc(done, 1)

            pool.memset(minus_half[:, :], -0.5)
            pool.memset(eps[:, :], EPS).then_inc(var_s, 1)
            pool.wait_ge(var_s, 1)
            rstd(0, 0, mv, rs, 2)
            with pool.Fori(0, tiles - 1) as t:
                rstd(0, t + 1, mv, rs, 2 * t + 3)
                rstd(1, t, mv2, rs2, 2 * t + 4)
            rstd(1, tiles - 1, mv2, rs2, 2 * tiles + 1)


def build(nc, args):
    layer_stack_moe(nc, *args)


def kernel(**inputs):
    import concourse.bacc as _bacc
    from concourse import mybir as _mybir
    from concourse.bass_utils import run_bass_kernel_spmd as _run

    a = {k.replace("L0_attn_", "").replace("L0_ffn_", ""): np.asarray(v) for k, v in inputs.items()}

    def by_channel(v):
        return v.reshape(LAYERS, HALVES, P, -1).transpose(2, 0, 1, 3)

    xp = a["x_proj_w"].transpose(0, 2, 1).reshape(LAYERS, HALVES, P, -1).transpose(2, 0, 1, 3)
    arrays = {
        "x": a["x"],
        "w_in": a["in_proj_w"].transpose(2, 0, 1),
        "w_bc": np.concatenate([xp[..., DT_RANK:]] * PARTS, axis=-1),
        "w_dt": xp[..., :DT_RANK],
        "w_delta": a["dt_proj_w"].transpose(2, 0, 1),
        "w_out": a["out_proj_w"].transpose(0, 2, 1).reshape(LAYERS, HALVES, P, D_MODEL).transpose(2, 0, 1, 3),
        "chan": np.concatenate([by_channel(a["conv_w"]), by_channel(a["conv_b"]), by_channel(a["dt_proj_b"]),
                                by_channel(a["D"])], axis=-1),
        "a_log": by_channel(a["A_log"]).reshape(P, -1),
        "sel": np.tile(np.eye(BC, dtype=np.float32), (PARTS, 1))[:, :, None].repeat(P, 2).astype(_mybir.dt.np(BF16)),
        "ident": np.eye(P, dtype=np.float32),
        "w_r": a["Wr"],
        "b_r": a["br"],
        "w1": a["W1"].transpose(1, 0, 2),
        "w2": a["W2"].reshape(EXPERTS, FCH, P, D_MODEL).transpose(2, 0, 1, 3),
    }
    nc = _bacc.Bacc("TRN2", target_bir_lowering=False, num_devices=1)
    feed, args = {}, []
    for name, v in arrays.items():
        v = np.ascontiguousarray(v)
        feed[f"in_{name}"] = v
        args.append(nc.dram_tensor(f"in_{name}", v.shape, _mybir.dt.from_np(v.dtype), kind="ExternalInput").ap())
    args.append(nc.dram_tensor("out", a["x"].shape, F32, kind="ExternalOutput").ap())
    build(nc, args)
    r = _run(nc, [feed], core_ids=[0])
    return r.results[0]["out"]
```

```python
from contextlib import ExitStack

import numpy as np

import concourse.bass as bass
from concourse import mybir

ALU = mybir.AluOpType
ACT = mybir.ActivationFunctionType
F32 = mybir.dt.float32
BF16 = mybir.dt.bfloat16
AX_X = mybir.AxisListType.X

P = 128
LAYERS, D_MODEL, D_INNER, D_STATE, D_CONV, DT_RANK = 4, 128, 256, 16, 4, 64
SEQ = 256
T = 512
SPT = T // SEQ
BLK = T // P
HALVES = D_INNER // P
EXPERTS, FFN = 8, 512
FCH = FFN // P
EPS = 1e-5
STREAMS = 4
ROUND = STREAMS * LAYERS
RING = 4
LAG = 3
AT_U, AT_Z, AT_SILU, AT_BC, AT_DT, AT_DELTA = 0, 2, 6, 7, 9, 10
AT_Y = 2
AT_IN, AT_OUT = 12, 13
BC = 2 * D_STATE
PARTS = 3
SIGMOID_ONE = float(25 * np.log(2.0))


def layer_stack_moe(nc, x, w_in, w_bc, w_dt, w_delta, w_out, chan, a_log, sel, ident, w_r, b_r, w1, w2, out):
    tiles = x.shape[0] * x.shape[1] // T
    steps = tiles * LAYERS
    x_t = x.rearrange("s (b p) d -> (s b) p d", p=P).rearrange("(t b) p d -> t p b d", b=BLK)
    out_t = out.rearrange("s (b p) d -> (s b) p d", p=P).rearrange("(t b) p d -> t p b d", b=BLK)

    with ExitStack() as ctx:
        def sb(name, shape, dt=F32):
            return ctx.enter_context(nc.sbuf_tensor(name, shape, dt))

        def bank(name):
            return ctx.enter_context(nc.psum_tensor(name, [P, 512], F32))

        def sem(name):
            return ctx.enter_context(nc.semaphore(name))

        w_in_sb = sb("w_in_sb", [P, LAYERS, 2 * D_INNER])
        w_bc_sb = sb("w_bc_sb", [P, LAYERS, HALVES, PARTS * BC])
        w_dt_sb = sb("w_dt_sb", [P, LAYERS, HALVES, DT_RANK])
        w_delta_sb = sb("w_delta_sb", [DT_RANK, LAYERS, D_INNER])
        w_out_sb = sb("w_out_sb", [P, LAYERS, HALVES, D_MODEL])
        chan_sb = sb("chan_sb", [P, LAYERS, HALVES, D_CONV + 3])
        a_sb = sb("a_sb", [P, LAYERS * HALVES * D_STATE])
        a_exp = sb("a_exp", [P, LAYERS * HALVES * D_STATE])
        sel_sb = sb("sel_sb", [PARTS * BC, BC, P], BF16)
        ident_sb = sb("ident_sb", [P, P])
        w_r_sb = sb("w_r_sb", [P, EXPERTS])
        b_r_sb = sb("b_r_sb", [P, EXPERTS])
        w1_sb = sb("w1_sb", [P, EXPERTS, FFN])
        w2_sb = sb("w2_sb", [P, EXPERTS, FCH, D_MODEL])
        residual = sb("residual", [P, tiles * BLK, D_MODEL])

        x_stage = sb("x_stage", [P, 2, BLK, D_MODEL])
        layer_in = sb("layer_in", [P, STREAMS, T])
        conv = sb("conv", [P, HALVES, T])
        u = sb("u", [P, 2, HALVES, T])
        z_gate = sb("z_gate", [P, 2, HALVES, T])
        bc_rest = sb("bc_rest", [PARTS * BC, T])
        bc_mid = sb("bc_mid", [PARTS * BC, T], BF16)
        bc_parts = sb("bc_parts", [PARTS * BC, 2, T], BF16)
        dt_rows = sb("dt_rows", [DT_RANK, T])
        sp_exp = sb("sp_exp", [P, HALVES, T])
        sp_relu = sb("sp_relu", [P, HALVES, T])
        delta = sb("delta", [P, 2, HALVES, T])
        du = sb("du", [P, 2, HALVES, T])
        dbu = sb("dbu", [P, 2, HALVES * T])
        h_state = sb("h_state", [P, RING, HALVES * T])
        c_bcast = sb("c_bcast", [P, 2, T])
        ch = sb("ch", [P, RING, HALVES, T])
        y_skip = sb("y_skip", [P, HALVES, T])
        gated = y_skip

        ps_b0, ps_b1, ps_c, ps_da0, ps_da1, ps_y0, ps_y1, ps_j = [bank(f"ps{i}") for i in range(8)]
        ps_b, ps_da, ps_y = [ps_b0, ps_b1], [ps_da0, ps_da1], [ps_y0, ps_y1]
        u_raw, z_raw = sp_relu, sp_exp

        x1 = u
        x1_t = layer_in
        hid = ch[:, :, :, :].rearrange("p (e r) h t -> p e (r h) t", e=2)
        moe = conv
        ln_stats = sb("ln_stats", [P, 2, BLK, 6])
        ln_mv = sb("ln_mv", [P, 2, BLK, 2])
        ln_rstd = sb("ln_rstd", [P, 2, BLK])
        var_eps = sb("var_eps", [P, 2, BLK])
        minus_half = sb("minus_half", [P, BLK])
        eps = sb("eps", [P, BLK])
        scratch = sb("scratch", [P, 1])
        lg = sb("lg", [P, BLK, EXPERTS])
        lg_max = sb("lg_max", [P, BLK])
        rank = sb("rank", [P, BLK, EXPERTS])
        prio = sb("prio", [P, BLK, EXPERTS])
        mask = sb("mask", [P, 2, BLK, EXPERTS])
        prob_t = sb("prob_t", [P, BLK])
        prob = sb("prob", [P, 2, BLK])

        names = ["w_loaded", "moe_loaded", "x_loaded0", "x_loaded1", "zeroed", "a_neg", "a_ready",
                 "in_mm", "out_mm", "u_mm", "z_mm", "bc_mm", "dt_mm", "delta_mm",
                 "b_ready", "c_ready", "y_mm",
                 "in_ready", "conv_init", "u_taken", "z_taken", "conv_tap", "conv_done",
                 "u_ready", "z_ready", "bc_hi", "bc_rest_s", "bc_mid_s", "bc_lo", "dt_ready",
                 "sp_abs", "sp_e", "sp_ln", "delta_ready", "du_ready",
                 "da_ready", "c_copied", "dbu_ready", "scanned", "ch_ready",
                 "y_taken", "gate_ready", "res_init", "res_done",
                 "st", "mv", "rs", "x1_ready", "xt_mm", "xt_ready", "lg_mm", "rt", "pr", "route_ready", "prob_ready", "var_s",
                 "hid_mm", "hid_ready", "ffn_mm", "ffn_taken", "moe_done", "fin", "st2", "mv2", "rs2", "o_ready", "stored0", "stored1"]
        S = {n: sem(n) for n in names}
        (w_loaded, moe_loaded, x_loaded0, x_loaded1, zeroed, a_neg, a_ready,
         in_mm, out_mm, u_mm, z_mm, bc_mm, dt_mm, delta_mm,
         b_ready, c_ready, y_mm,
         in_ready, conv_init, u_taken, z_taken, conv_tap, conv_done,
         u_ready, z_ready, bc_hi, bc_rest_s, bc_mid_s, bc_lo, dt_ready,
         sp_abs, sp_e, sp_ln, delta_ready, du_ready,
         da_ready, c_copied, dbu_ready, scanned, ch_ready,
         y_taken, gate_ready, res_init, res_done,
         st, mv, rs, x1_ready, xt_mm, xt_ready, lg_mm, rt, pr, route_ready, prob_ready, var_s,
         hid_mm, hid_ready, ffn_mm, ffn_taken, moe_done, fin, st2, mv2, rs2, o_ready, stored0, stored1) = [S[n] for n in names]

        x_loaded, stored = [x_loaded0, x_loaded1], [stored0, stored1]
        WEIGHT_DMAS, MOE_DMAS = 10, 3

        def wait(eng, s, count):
            if isinstance(count, int) and count <= 0:
                return
            eng.wait_ge(s, count)

        def run_steps(eng, step):
            for s in range(2):
                step(s, s)
            with eng.Fori(0, steps // ROUND - 1) as j:
                for k in range(2, 2 + ROUND):
                    step(j * ROUND + k, k)
            for s in range(steps - ROUND + 2, steps):
                step(s, s % ROUND)

        def is_step(s, value):
            return isinstance(s, int) and s == value

        def is_last(s, count=1):
            return isinstance(s, int) and s >= steps - count

        def layer_of(k):
            return k % ROUND // STREAMS

        def round_of(s, k):
            return s // ROUND if isinstance(s, int) else (s - k) // ROUND + k // ROUND

        def tile_of(s, k):
            return round_of(s, k) * STREAMS + k % STREAMS

        block = ctx.enter_context(nc.Block())

        @block.sync
        def _(sp):
            for dst, src in ((ident_sb[:, :], ident), (w_in_sb[:, :, :], w_in), (chan_sb[:, :, :, :], chan),
                             (w_bc_sb[:, :, :, :], w_bc), (w_dt_sb[:, :, :, :], w_dt),
                             (w_delta_sb[:, :, :], w_delta), (a_sb[:, :], a_log), (sel_sb[:, :, :], sel),
                             (w_out_sb[:, :, :, :], w_out), (w_r_sb[:, :], w_r)):
                sp.dma_start(dst, src).then_inc(w_loaded, 16)
            for t in range(2):
                sp.dma_start(x_stage[:, t], x_t[t]).then_inc(x_loaded[t], 16)
            sp.dma_start(w1_sb[:, :, :], w1).then_inc(moe_loaded, 16)
            sp.dma_start(w2_sb[:, :, :, :], w2).then_inc(moe_loaded, 16)
            sp.dma_start(b_r_sb[:, :], b_r.rearrange("(a e) -> a e", a=1).to_broadcast([P, EXPERTS])).then_inc(moe_loaded, 16)
            with sp.Fori(1, tiles // 2) as j:
                for half in range(2):
                    copied = sp.snap(j * 2 + (half - 1))
                    sp.wait_ge(w_loaded, 16 * WEIGHT_DMAS)
                    sp.wait_ge(res_init, copied)
                    sp.dma_start(x_stage[:, half], x_t[bass.ds(j * 2 + half, 1)].rearrange("t p b d -> (t p) b d")
                                 ).then_inc(x_loaded[half], 16)
            with sp.Fori(0, tiles // 2) as j:
                for half in range(2):
                    made = sp.snap(j * 2 + (half + 1))
                    sp.wait_ge(w_loaded, 16 * WEIGHT_DMAS)
                    sp.wait_ge(o_ready, made)
                    sp.dma_start(out_t[bass.ds(j * 2 + half, 1)].rearrange("t p b d -> (t p) b d"),
                                 z_gate[:, half, 0, :].rearrange("p (b d) -> p b d", b=BLK)).then_inc(stored[half], 16)
            for half in range(2):
                sp.wait_ge(stored[half], 16 * (tiles // 2))

        @block.tensor
        def _(pe):
            def project_in(p, k):
                if isinstance(p, int) and p < STREAMS - 1:
                    wait(pe, in_ready, p)
                else:
                    pe.wait_ge(sp_abs, 4 * (p - 1))
                if layer_of(k) == 0:
                    pe.wait_ge(x_loaded[k % 2], round_of(p, k) * 32 + (k % STREAMS // 2 + 1) * 16)
                    for b in range(BLK):
                        last = pe.transpose(ps_j[:, b * P:(b + 1) * P], x_stage[:, k % 2, b, :], ident_sb[:, :])
                else:
                    pe.wait_ge(gate_ready, p - STREAMS + 1)
                    for h in range(HALVES):
                        last = pe.matmul(ps_j[:, :], w_out_sb[:, layer_of(k) - 1, h, :], gated[:, h, :],
                                         start=(h == 0), stop=(h == HALVES - 1))
                last.then_inc(in_mm, 1)

            def project_out(s):
                pe.wait_ge(gate_ready, s + 1)
                if is_last(s, STREAMS):
                    pe.wait_ge(sp_abs, 4 * min(s + 3, steps))
                else:
                    pe.wait_ge(in_ready, s + STREAMS + 1)
                for b in range(BLK):
                    for h in range(HALVES):
                        last = pe.matmul(ps_j[:, b * P:(b + 1) * P], gated[:, h, b * P:(b + 1) * P],
                                         w_out_sb[:, LAYERS - 1, h, :], start=(h == 0), stop=(h == HALVES - 1))
                last.then_inc(out_mm, 1)

            def half_in(k, which, done):
                pe.matmul(ps_j[:, :], w_in_sb[:, layer_of(k), which * P:(which + 1) * P], layer_in[:, k % STREAMS, :],
                          start=True, stop=True).then_inc(done, 1)

            def project_u(p, k, h):
                if h == 0:
                    pe.wait_ge(in_ready, min(max(p + 2, STREAMS - 1), steps) if isinstance(p, int) else p + 2)
                    if layer_of(k - 3) == LAYERS - 1 and not (isinstance(p, int) and p < 3):
                        pe.wait_ge(res_done, tile_of(p - 3, k - 3) + 1)
                    else:
                        wait(pe, sp_abs, 4 * p)
                else:
                    pe.wait_ge(u_taken, 2 * p + 1)
                half_in(k, h, u_mm)

            def project_z(p, k, h):
                if h == 0:
                    pe.wait_ge(u_taken, 2 * p + 2)
                else:
                    pe.wait_ge(z_taken, 2 * p + 1)
                half_in(k, HALVES + h, z_mm)

            def project_bc(p, k):
                pe.wait_ge(u_ready, p + 1)
                pe.wait_ge(z_taken, 2 * p + 2)
                for h in range(HALVES):
                    last = pe.matmul(ps_j[0:PARTS * BC, :], w_bc_sb[:, layer_of(k), h, :], u[:, k % 2, h, :],
                                     start=(h == 0), stop=(h == HALVES - 1))
                last.then_inc(bc_mm, 1)

            def project_dt(p, k):
                pe.wait_ge(bc_rest_s, p + 1)
                for h in range(HALVES):
                    last = pe.matmul(ps_j[0:DT_RANK, :], w_dt_sb[:, layer_of(k), h, :], u[:, k % 2, h, :],
                                     start=(h == 0), stop=(h == HALVES - 1))
                last.then_inc(dt_mm, 1)

            def project_delta(p, k, h):
                if h == 0:
                    pe.wait_ge(dt_ready, p + 1)
                else:
                    pe.wait_ge(sp_abs, 4 * p + 2)
                pe.matmul(ps_j[:, :], w_delta_sb[:, layer_of(k), h * P:(h + 1) * P], dt_rows[:, :],
                          start=True, stop=True).then_inc(delta_mm, 1)

            def broadcast_b(s, k, n):
                q = s * D_STATE + n
                if n == 0:
                    pe.wait_ge(bc_lo, s + 1)
                wait(pe, dbu_ready, q - 1)
                pe.matmul(ps_b[n % 2][:, :], sel_sb[:, n, :], bc_parts[:, k % 2, :], start=True, stop=True).then_inc(b_ready, 1)

            def broadcast_c(s, k, n):
                wait(pe, c_copied, s * D_STATE + n)
                pe.matmul(ps_c[:, :], sel_sb[:, D_STATE + n, :], bc_parts[:, k % 2, :], start=True, stop=True).then_inc(c_ready, 1)

            def sum_states(s, n):
                q = s * D_STATE + n
                pe.wait_ge(ch_ready, q + 1)
                if n == 0:
                    wait(pe, y_taken, s)
                for h in range(HALVES):
                    last = pe.matmul(ps_y[h][:, :], ident_sb[:, :], ch[:, n % RING, h, :],
                                     start=(n == 0), stop=(n == D_STATE - 1))
                last.then_inc(y_mm, 1)

            def step(s, k):
                if is_step(s, 0):
                    broadcast_b(s, k, 0)
                for n in range(D_STATE):
                    if n + 1 < D_STATE:
                        broadcast_b(s, k, n + 1)
                    elif not is_last(s):
                        broadcast_b(s + 1, k + 1, 0)
                    if n < LAG and not is_step(s, 0):
                        sum_states(s - 1, D_STATE - LAG + n)
                    if n >= LAG:
                        sum_states(s, n - LAG)
                    broadcast_c(s, k, n)
                    if not is_last(s):
                        if n in (AT_U, AT_U + 1):
                            project_u(s + 1, k + 1, n - AT_U)
                        if n in (AT_Z, AT_Z + 1):
                            project_z(s + 1, k + 1, n - AT_Z)
                        if n == AT_BC:
                            project_bc(s + 1, k + 1)
                        if n == AT_DT:
                            project_dt(s + 1, k + 1)
                        if n in (AT_DELTA, AT_DELTA + 1):
                            project_delta(s + 1, k + 1, n - AT_DELTA)
                    if n == AT_IN and not is_last(s, STREAMS - 1):
                        project_in(s + STREAMS - 1, k + STREAMS - 1)
                    if n == AT_OUT and layer_of(k - 1) == LAYERS - 1 and not is_step(s, 0):
                        project_out(s - 1)

            pe.wait_ge(w_loaded, 16 * WEIGHT_DMAS)
            for p in range(STREAMS - 1):
                project_in(p, p)
            for h in range(HALVES):
                project_u(0, 0, h)
            for h in range(HALVES):
                project_z(0, 0, h)
            project_bc(0, 0)
            project_dt(0, 0)
            for h in range(HALVES):
                project_delta(0, 0, h)
            run_steps(pe, step)
            for n in range(D_STATE - LAG, D_STATE):
                sum_states(steps - 1, n)
            project_out(steps - 1)

            pe.wait_ge(moe_loaded, 16 * MOE_DMAS)
            pe.wait_ge(res_done, tiles)

            def prepare(t, half):
                pe.wait_ge(x1_ready, t + 1)
                wait(pe, xt_ready, t)
                for b in range(BLK):
                    last = pe.transpose(ps_b0[:, b * P:(b + 1) * P], x1[:, half, 0, b * P:(b + 1) * P], ident_sb[:, :])
                last.then_inc(xt_mm, 1)
                pe.wait_ge(xt_ready, t + 1)
                wait(pe, route_ready, t)
                for b in range(BLK):
                    last = pe.matmul(ps_c[:, b * EXPERTS:(b + 1) * EXPERTS], x1_t[:, half, b * P:(b + 1) * P], w_r_sb[:, :],
                                     start=True, stop=True)
                last.then_inc(lg_mm, 1)

            hid_banks = [ps_da0, ps_da1, ps_y0, ps_y1]
            ffn_banks = [ps_j, ps_b1]

            def up(t, half, e):
                c = t * EXPERTS + e
                for f in range(FCH):
                    wait(pe, hid_ready, (c - 1) * FCH + f + 1)
                    pe.matmul(hid_banks[f][:, :], w1_sb[:, e, f * P:(f + 1) * P], x1_t[:, half, :],
                              start=True, stop=True).then_inc(hid_mm, 1)

            def down(t, e):
                c = t * EXPERTS + e
                pe.wait_ge(hid_ready, (c + 1) * FCH)
                wait(pe, ffn_taken, c - 1)
                for b in range(BLK):
                    for f in range(FCH):
                        last = pe.matmul(ffn_banks[e % 2][:, b * P:(b + 1) * P], hid[:, e % 2, f, b * P:(b + 1) * P],
                                         w2_sb[:, e, f, :], start=(f == 0), stop=(f == FCH - 1))
                last.then_inc(ffn_mm, 1)

            def tile(t, half, ahead):
                up(t, half, 0)
                for e in range(EXPERTS):
                    if e + 1 < EXPERTS:
                        up(t, half, e + 1)
                    if e == 4 and ahead:
                        prepare(t + 1, 1 - half)
                    down(t, e)

            prepare(0, 0)
            tile(0, 0, True)
            tile(1, 1, True)
            with pe.Fori(1, tiles // 2 - 1) as j:
                tile(j * 2, 0, True)
                tile(j * 2 + 1, 1, True)
            tile(tiles - 2, 0, True)
            tile(tiles - 1, 1, False)

        @block.scalar
        def _(act):
            CONV_B, DELTA_B, SKIP = D_CONV, D_CONV + 1, D_CONV + 2

            def chan_of(k, h, c):
                return chan_sb[:, layer_of(k), h, c:c + 1]

            def take_in(p, k):
                act.wait_ge(in_mm, p + 1)
                act.copy(layer_in[:, k % STREAMS, :], ps_j[:, :]).then_inc(in_ready, 1)
                if layer_of(k) == 0:
                    act.copy(residual[:, bass.ds(tile_of(p, k) * BLK, BLK), :], x_stage[:, k % 2]
                             ).then_inc(res_init, 1)

            def take_u(p, k, h):
                if h == 0:
                    wait(act, delta_ready, p)
                act.wait_ge(u_mm, 2 * p + h + 1)
                act.activation(conv[:, h, :], ps_j[:, :], ACT.Identity, bias=chan_of(k, h, CONV_B),
                               scale=chan_of(k, h, D_CONV - 1)).then_inc(conv_init, 1)
                act.copy(u_raw[:, h, :], ps_j[:, :]).then_inc(u_taken, 1)

            def take_z(p, h):
                act.wait_ge(z_mm, 2 * p + h + 1)
                act.copy(z_raw[:, h, :], ps_j[:, :]).then_inc(z_taken, 1)

            def silus(p, k):
                act.wait_ge(conv_done, 2 * p + 2)
                wait(act, y_taken, p - 1)
                act.activation(u[:, k % 2], conv[:, :, :], ACT.Silu).then_inc(u_ready, 1)
                wait(act, gate_ready, p - 1)
                act.wait_ge(z_taken, 2 * p + 2)
                act.activation(z_gate[:, k % 2], z_raw[:, :, :], ACT.Silu).then_inc(z_ready, 1)
                act.preload_act_table_set("natural_log_exp_and_others")

            def split_high(p, k):
                act.wait_ge(bc_mm, p + 1)
                act.copy(bc_parts[:, k % 2, :], ps_j[0:PARTS * BC, :]).then_inc(bc_hi, 1)

            def take_dt(p, k):
                act.wait_ge(dt_mm, p + 1)
                act.copy(dt_rows[:, :], ps_j[0:DT_RANK, :]).then_inc(dt_ready, 1)

            def split_mid(p, k):
                act.wait_ge(bc_rest_s, p + 1)
                wait(act, bc_lo, p)
                act.copy(bc_mid[:, :], bc_rest[:, :]).then_inc(bc_mid_s, 1)

            def softplus_parts(p, k, h):
                if h == 0:
                    act.wait_ge(conv_done, 2 * p + 2)
                    act.wait_ge(z_ready, p + 1)
                act.wait_ge(delta_mm, 2 * p + h + 1)
                bias = chan_of(k, h, DELTA_B)
                act.activation(sp_exp[:, h, :], ps_j[:, :], ACT.Abs, bias=bias).then_inc(sp_abs, 1)
                act.activation(sp_relu[:, h, :], ps_j[:, :], ACT.Relu, bias=bias).then_inc(sp_abs, 1)

            def softplus_exp(p):
                act.wait_ge(sp_abs, 4 * (p + 1))
                act.activation(sp_exp[:, :, :], sp_exp[:, :, :], ACT.Exp, scale=-1.0).then_inc(sp_e, 1)

            def softplus_ln(p):
                act.wait_ge(sp_e, p + 1)
                act.activation(sp_exp[:, :, :], sp_exp[:, :, :], ACT.Ln, bias=1.0).then_inc(sp_ln, 1)

            def copy_c(s, n):
                q = s * D_STATE + n
                wait(act, ch_ready, q - 1)
                act.wait_ge(c_ready, q + 1)
                act.copy(c_bcast[:, n % 2, :], ps_c[:, :]).then_inc(c_copied, 1)

            def decay(s, k, n):
                q = s * D_STATE + n
                if n == 0:
                    act.wait_ge(delta_ready, s + 1)
                for h in range(HALVES):
                    wait(act, scanned, 2 * q - 1 + h)
                    col = (layer_of(k) * HALVES + h) * D_STATE + n
                    act.activation(ps_da[h][:, :].rearrange("p (s t) -> p s t", s=SPT)[:, :, 1:SEQ],
                                   delta[:, k % 2, h, :].rearrange("p (s t) -> p s t", s=SPT)[:, :, 1:SEQ],
                                   ACT.Exp, scale=a_sb[:, col:col + 1]).then_inc(da_ready, 1)

            def step(s, k):
                p, kp = s + 1, k + 1
                for n in range(D_STATE):
                    decay(s, k, n)
                    copy_c(s, n)
                    if not is_last(s):
                        if n in (AT_U, AT_U + 1):
                            take_u(p, kp, n - AT_U)
                        if n in (AT_Z, AT_Z + 1):
                            take_z(p, n - AT_Z)
                        if n == AT_SILU:
                            silus(p, kp)
                        if n == AT_BC:
                            split_high(p, kp)
                        if n == AT_BC + 1:
                            split_mid(p, kp)
                        if n == AT_DT:
                            take_dt(p, kp)
                        if n in (AT_DELTA, AT_DELTA + 1):
                            softplus_parts(p, kp, n - AT_DELTA)
                        if n == AT_DELTA + 2:
                            softplus_exp(p)
                            softplus_ln(p)
                    if n == AT_IN and not is_last(s, STREAMS - 1):
                        take_in(s + STREAMS - 1, k + STREAMS - 1)

            act.wait_ge(w_loaded, 16 * WEIGHT_DMAS)
            act.activation(a_exp[:, :], a_sb[:, :], ACT.Exp).then_inc(a_neg, 1)
            act.wait_ge(a_neg, 1)
            act.mul(a_sb[:, :], a_exp[:, :], -1.0).then_inc(a_ready, 1)
            for p in range(STREAMS - 1):
                take_in(p, p)
            for h in range(HALVES):
                take_u(0, 0, h)
            for h in range(HALVES):
                take_z(0, h)
            silus(0, 0)
            split_high(0, 0)
            split_mid(0, 0)
            take_dt(0, 0)
            for h in range(HALVES):
                softplus_parts(0, 0, h)
            softplus_exp(0)
            softplus_ln(0)
            act.wait_ge(a_ready, 1)
            act.wait_ge(zeroed, 2)
            run_steps(act, step)

            hid_banks = [ps_da0, ps_da1, ps_y0, ps_y1]

            def prepare(t, half):
                act.wait_ge(xt_mm, t + 1)
                act.copy(x1_t[:, half, :], ps_b0[:, :]).then_inc(xt_ready, 1)
                act.wait_ge(rt, 6 * t + 3)
                act.activation(prob_t[:, :], lg_max[:, :], ACT.Tanh, scale=0.5).then_inc(pr, 1)

            def gelu(t, e):
                c = t * EXPERTS + e
                wait(act, ffn_mm, c - 1)
                for f in range(FCH):
                    act.wait_ge(hid_mm, c * FCH + f + 1)
                    act.activation(hid[:, e % 2, f, :], hid_banks[f][:, :], ACT.Gelu).then_inc(hid_ready, 1)

            def tile(t, half, ahead):
                gelu(t, 0)
                for e in range(EXPERTS):
                    if e + 1 < EXPERTS:
                        gelu(t, e + 1)
                    if e == 4 and ahead:
                        prepare(t + 1, 1 - half)

            prepare(0, 0)
            tile(0, 0, True)
            tile(1, 1, True)
            with act.Fori(1, tiles // 2 - 1) as j:
                tile(j * 2, 0, True)
                tile(j * 2 + 1, 1, True)
            tile(tiles - 2, 0, True)
            tile(tiles - 1, 1, False)

        @block.vector
        def _(dve):
            SKIP = D_CONV + 2

            def conv_taps(p, k, shift, h):
                src = u_raw[:, h, :].rearrange("p (s t) -> p s t", s=SPT)[:, :, 0:SEQ - shift]
                acc = conv[:, h, :].rearrange("p (s t) -> p s t", s=SPT)[:, :, shift:SEQ]
                if shift == 1:
                    dve.wait_ge(u_taken, 2 * p + h + 1)
                else:
                    dve.wait_ge(conv_tap, 4 * p + 2 * (shift - 2) + h + 1)
                tap = dve.scalar_tensor_tensor(acc, src, chan_sb[:, layer_of(k), h, D_CONV - 1 - shift:D_CONV - shift], acc,
                                               ALU.mult, ALU.add)
                if shift < D_CONV - 1:
                    tap.then_inc(conv_tap, 1)
                else:
                    tap.then_inc(conv_done, 1)

            def split_rest(p, k):
                dve.wait_ge(bc_hi, p + 1)
                wait(dve, bc_mid_s, p)
                dve.tensor_tensor(bc_rest[:, :], ps_j[0:PARTS * BC, :], bc_parts[:, k % 2, :], ALU.subtract
                                  ).then_inc(bc_rest_s, 1)

            def split_low(p, k):
                dve.wait_ge(bc_mid_s, p + 1)
                dve.tensor_copy(bc_parts[BC:2 * BC, k % 2, :], bc_mid[BC:2 * BC, :])
                dve.tensor_tensor(bc_parts[2 * BC:3 * BC, k % 2, :], bc_rest[2 * BC:3 * BC, :], bc_mid[2 * BC:3 * BC, :],
                                  ALU.subtract).then_inc(bc_lo, 1)

            def make_delta(p, k):
                dve.wait_ge(sp_ln, p + 1)
                dve.tensor_tensor(delta[:, k % 2], sp_relu[:, :, :], sp_exp[:, :, :], ALU.add).then_inc(delta_ready, 1)

            def take_y(s, k):
                dve.wait_ge(y_mm, (s + 1) * D_STATE)
                if not is_step(s, 0):
                    if layer_of(k - 1) == LAYERS - 1:
                        dve.wait_ge(out_mm, tile_of(s - 1, k - 1) + 1)
                    else:
                        dve.wait_ge(in_mm, s + STREAMS)
                for h in range(HALVES):
                    last = dve.scalar_tensor_tensor(y_skip[:, h, :], u[:, k % 2, h, :], chan_sb[:, layer_of(k), h, SKIP:SKIP + 1],
                                                    ps_y[h][:, :], ALU.mult, ALU.add)
                last.then_inc(y_taken, 1)

            def add_residual(s, k):
                t = tile_of(s, k)
                dve.wait_ge(out_mm, t + 1)
                dve.wait_ge(res_init, t + 1)
                rows = residual[:, bass.ds(t * BLK, BLK), :]
                dve.tensor_tensor(rows, ps_j[:, :].rearrange("p (b d) -> p b d", b=BLK), rows, ALU.add).then_inc(res_done, 1)

            def inputs(s, k, n):
                q = s * D_STATE + n
                if n == 0:
                    dve.wait_ge(du_ready, s + 1)
                dve.wait_ge(b_ready, q + 1)
                wait(dve, scanned, 2 * (q - 1))
                dve.tensor_tensor(dbu[:, n % 2, :].rearrange("p (h t) -> p h t", h=HALVES), du[:, k % 2],
                                  ps_b[n % 2][:, :].unsqueeze(1).to_broadcast([P, HALVES, T]), ALU.mult).then_inc(dbu_ready, 1)

            def scan(s, n):
                q = s * D_STATE + n
                dve.wait_ge(dbu_ready, q + 1)
                wait(dve, ch_ready, q - RING + 1)
                for h in range(HALVES):
                    dve.wait_ge(da_ready, 2 * q + h + 1)
                    dve.tensor_tensor_scan(h_state[:, n % RING, h * T:(h + 1) * T], ps_da[h][:, :],
                                           dbu[:, n % 2, h * T:(h + 1) * T], 0.0, ALU.mult, ALU.add).then_inc(scanned, 1)

            CONV_AT = {2: ((1, 0),), 3: ((1, 1), (2, 0)), 4: ((2, 1), (3, 0)), 5: ((3, 1),)}

            def step(s, k):
                if is_step(s, 0):
                    inputs(s, k, 0)
                for n in range(D_STATE):
                    if n + 1 < D_STATE:
                        inputs(s, k, n + 1)
                    scan(s, n)
                    if n == AT_Y and not is_step(s, 0):
                        take_y(s - 1, k - 1)
                    if not is_last(s):
                        for shift, h in CONV_AT.get(n, ()):
                            conv_taps(s + 1, k + 1, shift, h)
                        if n == AT_BC:
                            split_rest(s + 1, k + 1)
                        if n == AT_BC + 1:
                            split_low(s + 1, k + 1)
                    if n == AT_DELTA + 3 and not is_last(s):
                        make_delta(s + 1, k + 1)
                    if n == AT_OUT and layer_of(k - 1) == LAYERS - 1 and not is_step(s, 0):
                        add_residual(s - 1, k - 1)
                if not is_last(s):
                    inputs(s + 1, k + 1, 0)

            dve.memset(ps_da0[:, :], 0.0).then_inc(zeroed, 1)
            dve.memset(ps_da1[:, :], 0.0).then_inc(zeroed, 1)
            dve.wait_ge(w_loaded, 16 * WEIGHT_DMAS)
            for shift in (1, 2, 3):
                for h in range(HALVES):
                    conv_taps(0, 0, shift, h)
            split_rest(0, 0)
            split_low(0, 0)
            make_delta(0, 0)
            run_steps(dve, step)
            take_y(steps - 1, ROUND - 1)
            add_residual(steps - 1, ROUND - 1)

            ffn_banks = [ps_j, ps_b1]

            def blocks(ap):
                return ap.rearrange("p (b d) -> p b d", b=BLK)

            def norm_in(t, half):
                for b in range(BLK):
                    last = dve.bn_stats(ln_stats[:, 0, b, :], residual[:, bass.ds(t * BLK + b, 1), :].rearrange("p a d -> p (a d)"))
                last.then_inc(st, 1)
                dve.wait_ge(st, t + 1)
                dve.memset(scratch[:, :], 0.0)
                for b in range(BLK):
                    last = dve.bn_aggr(ln_mv[:, 0, b, :], ln_stats[:, 0, b, :])
                last.then_inc(mv, 1)
                dve.wait_ge(rs, t + 1)
                for b in range(BLK):
                    last = dve.tensor_scalar(x1[:, half, 0, b * P:(b + 1) * P],
                                             residual[:, bass.ds(t * BLK + b, 1), :].rearrange("p a d -> p (a d)"),
                                             ln_mv[:, 0, b, 0:1], ln_rstd[:, 0, b:b + 1], ALU.subtract, ALU.mult)
                last.then_inc(x1_ready, 1)

            def route(t, half):
                dve.wait_ge(lg_mm, t + 1)
                dve.tensor_tensor(lg[:, :, :], ps_c[:, 0:BLK * EXPERTS].rearrange("p (b e) -> p b e", b=BLK),
                                  b_r_sb[:, :].unsqueeze(1).to_broadcast([P, BLK, EXPERTS]), ALU.add).then_inc(rt, 1)
                dve.wait_ge(rt, 6 * t + 1)
                dve.tensor_scalar(lg[:, :, :], lg[:, :, :], SIGMOID_ONE, None, ALU.min).then_inc(rt, 1)
                dve.wait_ge(rt, 6 * t + 2)
                wait(dve, pr, t)
                dve.tensor_reduce(lg_max[:, :], lg[:, :, :], AX_X, ALU.max).then_inc(rt, 1)
                dve.wait_ge(rt, 6 * t + 3)
                dve.tensor_tensor(rank[:, :, :], lg[:, :, :], lg_max[:, :].unsqueeze(2).to_broadcast([P, BLK, EXPERTS]),
                                  ALU.is_equal).then_inc(rt, 1)
                dve.wait_ge(rt, 6 * t + 4)
                dve.tensor_tensor(rank[:, :, :], rank[:, :, :], prio[:, :, :], ALU.mult).then_inc(rt, 1)
                dve.wait_ge(rt, 6 * t + 5)
                dve.tensor_reduce(prob[:, half, :], rank[:, :, :], AX_X, ALU.max).then_inc(rt, 1)
                dve.wait_ge(rt, 6 * t + 6)
                dve.tensor_tensor(mask[:, half], rank[:, :, :], prob[:, half, :].unsqueeze(2).to_broadcast([P, BLK, EXPERTS]),
                                  ALU.is_equal).then_inc(route_ready, 1)
                dve.wait_ge(route_ready, t + 1)
                dve.wait_ge(pr, t + 1)
                dve.tensor_scalar(prob[:, half, :], prob_t[:, :], 0.5, 0.5, ALU.mult, ALU.add).then_inc(prob_ready, 1)

            def combine(t, half, e):
                c = t * EXPERTS + e
                dve.wait_ge(ffn_mm, c + 1)
                wait(dve, ffn_taken, c)
                for b in range(BLK):
                    cols = slice(b * P, (b + 1) * P)
                    m = mask[:, half, b, e:e + 1]
                    if e == 0:
                        last = dve.tensor_scalar(moe[:, 0, cols], ffn_banks[e % 2][:, cols], m, None, ALU.mult)
                    else:
                        last = dve.scalar_tensor_tensor(moe[:, 0, cols], ffn_banks[e % 2][:, cols], m, moe[:, 0, cols],
                                                        ALU.mult, ALU.add)
                last.then_inc(ffn_taken, 1)

            def finish(t, half):
                dve.wait_ge(ffn_taken, (t + 1) * EXPERTS)
                dve.wait_ge(prob_ready, t + 1)
                for b in range(BLK):
                    cols = slice(b * P, (b + 1) * P)
                    last = dve.scalar_tensor_tensor(moe[:, 1, cols], moe[:, 0, cols], prob[:, half, b:b + 1],
                                                    x1[:, half, 0, cols], ALU.mult, ALU.add)
                last.then_inc(fin, 1)
                dve.wait_ge(fin, t + 1)
                for b in range(BLK):
                    last = dve.bn_stats(ln_stats[:, 1, b, :], moe[:, 1, b * P:(b + 1) * P])
                last.then_inc(st2, 1)
                dve.wait_ge(st2, t + 1)
                dve.memset(scratch[:, :], 0.0)
                for b in range(BLK):
                    last = dve.bn_aggr(ln_mv[:, 1, b, :], ln_stats[:, 1, b, :])
                last.then_inc(mv2, 1)
                dve.wait_ge(rs2, t + 1)
                wait(dve, stored[half], 8 * (t - half))
                for b in range(BLK):
                    cols = slice(b * P, (b + 1) * P)
                    last = dve.tensor_scalar(z_gate[:, half, 0, cols], moe[:, 1, cols], ln_mv[:, 1, b, 0:1],
                                             ln_rstd[:, 1, b:b + 1], ALU.subtract, ALU.mult)
                last.then_inc(o_ready, 1)

            def tile(t, half, ahead):
                for e in range(EXPERTS):
                    if e == 2 and ahead:
                        norm_in(t + 1, 1 - half)
                    combine(t, half, e)
                    if e == 5 and ahead:
                        route(t + 1, 1 - half)
                finish(t, half)

            dve.wait_ge(moe_loaded, 16 * MOE_DMAS)
            dve.wait_ge(res_done, tiles)
            for e in range(EXPERTS):
                last = dve.memset(prio[:, :, e:e + 1], float(EXPERTS - e))
            last.then_inc(zeroed, 1)
            dve.wait_ge(zeroed, 3)
            norm_in(0, 0)
            route(0, 0)
            tile(0, 0, True)
            tile(1, 1, True)
            with dve.Fori(1, tiles // 2 - 1) as j:
                tile(j * 2, 0, True)
                tile(j * 2 + 1, 1, True)
            tile(tiles - 2, 0, True)
            tile(tiles - 1, 1, False)

        @block.gpsimd
        def _(pool):
            def make_du(p, k):
                pool.wait_ge(delta_ready, p + 1)
                pool.wait_ge(u_ready, p + 1)
                pool.tensor_tensor(du[:, k % 2], delta[:, k % 2], u[:, k % 2], ALU.mult).then_inc(du_ready, 1)

            def gate(s, k):
                pool.wait_ge(y_taken, s + 1)
                pool.wait_ge(z_ready, s + 1)
                pool.tensor_tensor(gated[:, :, :], y_skip[:, :, :], z_gate[:, k % 2], ALU.mult).then_inc(gate_ready, 1)

            def weigh(s, n):
                q = s * D_STATE + n
                pool.wait_ge(scanned, 2 * (q + 1))
                pool.wait_ge(c_copied, q + 1)
                wait(pool, y_mm, q - RING + 1)
                pool.tensor_tensor(ch[:, n % RING], h_state[:, n % RING, :].rearrange("p (h t) -> p h t", h=HALVES),
                                   c_bcast[:, n % 2, :].unsqueeze(1).to_broadcast([P, HALVES, T]), ALU.mult
                                   ).then_inc(ch_ready, 1)

            def step(s, k):
                for n in range(D_STATE):
                    weigh(s, n)
                    if n == AT_Y and not is_step(s, 0):
                        gate(s - 1, k - 1)
                    if n == AT_DELTA + 3 and not is_last(s):
                        make_du(s + 1, k + 1)

            make_du(0, 0)
            run_steps(pool, step)
            gate(steps - 1, ROUND - 1)

            def rstd(which, t, have, done, nth):
                pool.wait_ge(have, t + 1)
                pool.tensor_tensor(var_eps[:, which, :], ln_mv[:, which, :, 1], eps[:, :], ALU.add).then_inc(var_s, 1)
                pool.wait_ge(var_s, nth)
                pool.tensor_tensor(ln_rstd[:, which, :], var_eps[:, which, :], minus_half[:, :], ALU.pow).then_inc(done, 1)

            pool.memset(minus_half[:, :], -0.5)
            pool.memset(eps[:, :], EPS).then_inc(var_s, 1)
            pool.wait_ge(var_s, 1)
            rstd(0, 0, mv, rs, 2)
            with pool.Fori(0, tiles - 1) as t:
                rstd(0, t + 1, mv, rs, 2 * t + 3)
                rstd(1, t, mv2, rs2, 2 * t + 4)
            rstd(1, tiles - 1, mv2, rs2, 2 * tiles + 1)


def build(nc, args):
    layer_stack_moe(nc, *args)


def kernel(**inputs):
    import concourse.bacc as _bacc
    from concourse import mybir as _mybir
    from concourse.bass_utils import run_bass_kernel_spmd as _run

    a = {k.replace("L0_attn_", "").replace("L0_ffn_", ""): np.asarray(v) for k, v in inputs.items()}

    def by_channel(v):
        return v.reshape(LAYERS, HALVES, P, -1).transpose(2, 0, 1, 3)

    xp = a["x_proj_w"].transpose(0, 2, 1).reshape(LAYERS, HALVES, P, -1).transpose(2, 0, 1, 3)
    arrays = {
        "x": a["x"],
        "w_in": a["in_proj_w"].transpose(2, 0, 1),
        "w_bc": np.concatenate([xp[..., DT_RANK:]] * PARTS, axis=-1),
        "w_dt": xp[..., :DT_RANK],
        "w_delta": a["dt_proj_w"].transpose(2, 0, 1),
        "w_out": a["out_proj_w"].transpose(0, 2, 1).reshape(LAYERS, HALVES, P, D_MODEL).transpose(2, 0, 1, 3),
        "chan": np.concatenate([by_channel(a["conv_w"]), by_channel(a["conv_b"]), by_channel(a["dt_proj_b"]),
                                by_channel(a["D"])], axis=-1),
        "a_log": by_channel(a["A_log"]).reshape(P, -1),
        "sel": np.tile(np.eye(BC, dtype=np.float32), (PARTS, 1))[:, :, None].repeat(P, 2).astype(_mybir.dt.np(BF16)),
        "ident": np.eye(P, dtype=np.float32),
        "w_r": a["Wr"],
        "b_r": a["br"],
        "w1": a["W1"].transpose(1, 0, 2),
        "w2": a["W2"].reshape(EXPERTS, FCH, P, D_MODEL).transpose(2, 0, 1, 3),
    }
    nc = _bacc.Bacc("TRN2", target_bir_lowering=False, num_devices=1)
    feed, args = {}, []
    for name, v in arrays.items():
        v = np.ascontiguousarray(v)
        feed[f"in_{name}"] = v
        args.append(nc.dram_tensor(f"in_{name}", v.shape, _mybir.dt.from_np(v.dtype), kind="ExternalInput").ap())
    args.append(nc.dram_tensor("out", a["x"].shape, F32, kind="ExternalOutput").ap())
    build(nc, args)
    r = _run(nc, [feed], core_ids=[0])
    return r.results[0]["out"]
```

```python
from contextlib import ExitStack

import numpy as np

import concourse.bass as bass
from concourse import mybir

ALU = mybir.AluOpType
ACT = mybir.ActivationFunctionType
F32 = mybir.dt.float32
BF16 = mybir.dt.bfloat16
I32 = mybir.dt.int32
AX_X = mybir.AxisListType.X

P = 128
LAYERS, D_MODEL, D_INNER, D_STATE, D_CONV, DT_RANK = 4, 128, 256, 16, 4, 64
SEQ = 256
T = 512
SPT = T // SEQ
BLK = T // P
HALVES = D_INNER // P
EXPERTS, FFN = 8, 512
FCH = FFN // P
EPS = 1e-5
STREAMS = 4
ROUND = STREAMS * LAYERS
RING = 4
LAG = 3
AT_U, AT_Z = 0, 2
AT_SILU, AT_SILU_Z = 4, 5
AT_X, AT_HIGH = 6, 6
AT_REST, AT_MID, AT_REST2, AT_LOW = 7, 7, 8, 8
AT_DELTA = 9
AT_EXP, AT_LN = 11, 12
AT_SUM, AT_DU = 13, 13
AT_Y = 2
AT_OUT, AT_RESIDUAL = 14, 14
AT_IN, AT_TAKE_IN = 12, 13
EARLY = (5, 6)
DECAYS_BY = {4: 6}
BC = 2 * D_STATE
DT_ROWS = slice(2 * BC, P)
GROUP = 4
PARTS_OF_NORM = 2
HAND_OVER = 4
PARTS = 3
SIGMOID_ONE = float(25 * np.log(2.0))


def sorted_blocks_of(blocks):
    return -(-(blocks + EXPERTS - 1) // (2 * GROUP)) * 2 * GROUP


def layer_stack_moe(nc, x, w_in, w_x, w_delta, w_out, chan, a_log, sel, minus, ident, w_r, b_r, order, w1, w2, out):
    tiles = x.shape[0] * x.shape[1] // T
    steps = tiles * LAYERS
    blocks = tiles * BLK
    sorted_blocks = sorted_blocks_of(blocks)
    groups = sorted_blocks // GROUP
    sorted_x = nc.dram_tensor("sorted_x", [sorted_blocks * P, D_MODEL], F32)
    sorted_y = nc.dram_tensor("sorted_y", [sorted_blocks * P, D_MODEL], F32)
    sorted_x_g = sorted_x.ap().rearrange("(g b p) d -> g p b d", b=GROUP, p=P)
    sorted_y_g = sorted_y.ap().rearrange("(g b p) d -> g p b d", b=GROUP, p=P)
    x_t = x.rearrange("s (b p) d -> (s b) p d", p=P).rearrange("(t b) p d -> t p b d", b=BLK)
    out_t = out.rearrange("s (b p) d -> (s b) p d", p=P).rearrange("(t b) p d -> t p b d", b=BLK)

    with ExitStack() as ctx:
        def sb(name, shape, dt=F32):
            return ctx.enter_context(nc.sbuf_tensor(name, shape, dt))

        def bank(name):
            return ctx.enter_context(nc.psum_tensor(name, [P, 512], F32))

        def sem(name):
            return ctx.enter_context(nc.semaphore(name))

        w_in_sb = sb("w_in_sb", [P, LAYERS, 2 * D_INNER])
        w_x_sb = sb("w_x_sb", [P, LAYERS, HALVES, 2 * BC + DT_RANK])
        w_delta_sb = sb("w_delta_sb", [P, LAYERS, D_INNER])
        w_out_sb = sb("w_out_sb", [P, LAYERS, HALVES, D_MODEL])
        chan_sb = sb("chan_sb", [P, LAYERS, HALVES, D_CONV + 3])
        a_sb = sb("a_sb", [P, LAYERS * HALVES * D_STATE])
        a_exp = sb("a_exp", [P, LAYERS * HALVES * D_STATE])
        sel_sb = sb("sel_sb", [PARTS * BC, BC, P], BF16)
        ident_sb = sb("ident_sb", [P, P])
        w_r_sb = sb("w_r_sb", [P, EXPERTS])
        b_r_sb = sb("b_r_sb", [P, EXPERTS])
        zero_rows = sb("zero_rows", [P, D_MODEL])
        residual = sb("residual", [P, tiles * BLK, D_MODEL])

        x_stage = sb("x_stage", [P, 2, BLK, D_MODEL])
        layer_in = sb("layer_in", [P, STREAMS, T])
        conv = sb("conv", [P, HALVES, T])
        u = sb("u", [P, 2, HALVES, T])
        z_gate = sb("z_gate", [P, 2, HALVES, T])
        minus_sb = sb("minus_sb", [2 * BC, P], BF16)
        bc_parts = sb("bc_parts", [PARTS * BC, 2, T], BF16)
        dt_rows = sb("dt_rows", [P, T])
        sp_exp = sb("sp_exp", [P, HALVES, T])
        sp_relu = sb("sp_relu", [P, HALVES, T])
        u_raw = sb("u_raw", [P, HALVES, T])
        decays = sb("decays", [P, 2, HALVES * T])
        delta = sb("delta", [P, 2, HALVES, T])
        du = sb("du", [P, 2, HALVES, T])
        dbu = sb("dbu", [P, RING, HALVES * T])
        h_state = sb("h_state", [P, RING, HALVES * T])
        c_bcast = sb("c_bcast", [P, RING, T])
        ch = sb("ch", [P, RING, HALVES, T])
        y_skip = sb("y_skip", [P, HALVES, T])
        gated = y_skip

        ps_b0, ps_b1, ps_c, ps_da0, ps_da1, ps_y0, ps_y1, ps_j = [bank(f"ps{i}") for i in range(8)]
        ps_b, ps_da, ps_y = [ps_b0, ps_b1], [ps_da0, ps_da1], [ps_y0, ps_y1]
        z_raw = sp_exp

        def blocks_of(ap):
            return ap.rearrange("p (b e) -> p b e", e=EXPERTS)

        def experts_of(ap):
            return ap.rearrange("p (e b) -> p e b", e=EXPERTS)

        x1 = residual
        x1_t = [layer_in[:, i] for i in range(2)]
        sorted_in = [u[:, i, 0] for i in range(2)]
        sorted_t = [layer_in[:, 2 + i] for i in range(2)]
        w1_sb = h_state[:, :, :].rearrange("p e f -> p (e f)").rearrange("p (e f) -> p e f", e=EXPERTS)
        w2_sb = ch[:, :, :, :].rearrange("p r h t -> p (r h t)").rearrange("p (e f) -> p e f", e=EXPERTS)
        weights = [du[:, i].rearrange("p h t -> p (h t)") for i in range(2)] + [dbu[:, i] for i in range(2)]
        hid = [conv[:, i] for i in range(2)]
        y_stage = [u[:, i, 1] for i in range(2)]
        y_back = [decays[:, i // 2, i % 2 * T:(i % 2 + 1) * T] for i in range(HAND_OVER)]
        x2 = [delta[:, i // 2, i % 2] for i in range(HAND_OVER)]
        out_stage = [z_gate[:, i, 0] for i in range(2)]
        order_sb = x_stage[:, 0].rearrange("p b d -> p (b d)")
        before, ones = order_sb[:, 0:P], order_sb[:, P:2 * P]
        fills = order_sb[:, 2 * P:2 * P + blocks]
        numbers = order_sb[:, 2 * P + blocks:2 * P + blocks + sorted_blocks]
        lg, rank = du[:, 0, 0], du[:, 0, 1]
        mask, cum = du[:, 1, 0], du[:, 1, 1]
        at_pos, keep = dbu[:, 0, 0:T], dbu[:, 1, 0:T]
        prio = y_skip[:, 0]
        ended = c_bcast[:, :, :].rearrange("p a t -> p (a t)")[:, 0:sorted_blocks * EXPERTS]
        wide = z_gate[:, 0, 1]
        ln_stats = wide[:, 0:6 * blocks].rearrange("p (b c) -> p b c", c=6)
        ln_stats2 = wide[:, 6 * blocks:6 * blocks + 6 * HAND_OVER * BLK].rearrange("p (i b c) -> p i b c", i=HAND_OVER, c=6)
        narrow = z_gate[:, 1, 1].rearrange("p (a b) -> p a b", b=blocks)
        ln_mv = z_gate[:, 1, 1, 0:2 * blocks].rearrange("p (b c) -> p b c", c=2)
        ln_rstd, var_eps, minus_half, eps, lg_max, prob_t = [narrow[:, i] for i in range(2, 8)]
        small = x_stage[:, 1].rearrange("p b d -> p (b d)")
        ln_mv2 = small[:, 0:2 * HAND_OVER * BLK].rearrange("p (i b c) -> p i b c", i=HAND_OVER, c=2)
        ln_rstd2 = small[:, P:P + HAND_OVER * BLK].rearrange("p (i b) -> p i b", i=HAND_OVER)
        var_eps2 = small[:, 2 * P:2 * P + HAND_OVER * BLK].rearrange("p (i b) -> p i b", i=HAND_OVER)
        total, padded, end, base, ones_e = [small[:, 3 * P + EXPERTS * i:3 * P + EXPERTS * (i + 1)] for i in range(5)]
        scratch = sb("scratch", [P, 1])
        prob = sb("prob", [P, blocks])
        pos = sb("pos", [P, blocks])
        row_of = sb("row_of", [P, blocks], I32)
        ended_n = sb("ended_n", [P, sorted_blocks])
        expert_of = sb("expert_of", [P, sorted_blocks], I32)

        names = ["w_loaded", "bias_loaded", "x_loaded0", "x_loaded1", "zeroed", "a_neg", "a_ready",
                 "in_mm", "out_mm", "u_mm", "z_mm", "x_mm", "delta_mm",
                 "b_ready", "c_ready", "y_mm",
                 "in_ready", "conv_init", "u_taken", "z_taken", "conv_tap", "conv_done",
                 "u_ready", "z_ready", "bc_hi", "rest_mm", "bc_mid_s", "bc_lo", "dt_ready",
                 "sp_abs", "sp_e", "sp_ln", "delta_ready", "du_ready",
                 "da_ready", "c_copied", "dbu_ready", "scanned", "ch_ready",
                 "y_taken", "gate_ready", "residual_loaded", "res_done",
                 "stats", "mv", "centred", "var_s", "rstd_s", "consts_set", "x1_ready", "xt_mm", "xt_ready", "lg_mm", "routed",
                 "tanh_s", "prob_ready", "order_loaded", "experts_loaded", "pad_zeroed", "count_mm", "placed",
                 "row_ready", "expert_ready", "scattered", "sorted_loaded0", "sorted_loaded1", "st_mm", "st_ready",
                 "weights_ready", "up_mm", "gelu_s", "down_mm", "y_copied", "y_stored0", "y_stored1",
                 "gathered0", "gathered1", "gathered2", "gathered3",
                 "x2_ready", "stats2", "mv2", "var2_s", "rstd2_s", "o_ready", "stored0", "stored1"]
        (w_loaded, bias_loaded, x_loaded0, x_loaded1, zeroed, a_neg, a_ready,
         in_mm, out_mm, u_mm, z_mm, x_mm, delta_mm,
         b_ready, c_ready, y_mm,
         in_ready, conv_init, u_taken, z_taken, conv_tap, conv_done,
         u_ready, z_ready, bc_hi, rest_mm, bc_mid_s, bc_lo, dt_ready,
         sp_abs, sp_e, sp_ln, delta_ready, du_ready,
         da_ready, c_copied, dbu_ready, scanned, ch_ready,
         y_taken, gate_ready, residual_loaded, res_done,
         stats, mv, centred, var_s, rstd_s, consts_set, x1_ready, xt_mm, xt_ready, lg_mm, routed,
         tanh_s, prob_ready, order_loaded, experts_loaded, pad_zeroed, count_mm, placed,
         row_ready, expert_ready, scattered, sorted_loaded0, sorted_loaded1, st_mm, st_ready,
         weights_ready, up_mm, gelu_s, down_mm, y_copied, y_stored0, y_stored1,
         gathered0, gathered1, gathered2, gathered3,
         x2_ready, stats2, mv2, var2_s, rstd2_s, o_ready, stored0, stored1) = [sem(n) for n in names]

        x_loaded, stored = [x_loaded0, x_loaded1], [stored0, stored1]
        sorted_loaded, y_stored = [sorted_loaded0, sorted_loaded1], [y_stored0, y_stored1]
        gathered = [gathered0, gathered1, gathered2, gathered3]
        WEIGHT_DMAS = 10
        MAX_FOUND = 3
        COUNTED = 1
        BEHIND = 2
        hid_banks, y_banks = [ps_da0, ps_da1], [ps_y0, ps_y1]

        def wait(eng, s, count):
            if isinstance(count, int) and count <= 0:
                return
            eng.wait_ge(s, count)

        def run_steps(eng, step):
            for s in range(2):
                step(s, s)
            with eng.Fori(0, steps // ROUND - 1) as j:
                for k in range(2, 2 + ROUND):
                    step(j * ROUND + k, k)
            for s in range(steps - ROUND + 2, steps):
                step(s, s % ROUND)

        def decay_buffer(n, h):
            if n in EARLY:
                return decays[:, EARLY.index(n) % 2, h * T:(h + 1) * T]
            return ps_da[h][:, :]

        def last_user(n):
            same = [m for m in range(D_STATE) if decay_buffer_of(m) == decay_buffer_of(n)]
            i = same.index(n)
            return same[i - 1] - (D_STATE if i == 0 else 0)

        def decay_buffer_of(n):
            return EARLY.index(n) % 2 if n in EARLY else None

        def is_step(s, value):
            return isinstance(s, int) and s == value

        def is_last(s, count=1):
            return isinstance(s, int) and s >= steps - count

        def layer_of(k):
            return k % ROUND // STREAMS

        def round_of(s, k):
            return s // ROUND if isinstance(s, int) else (s - k) // ROUND + k // ROUND

        def tile_of(s, k):
            return round_of(s, k) * STREAMS + k % STREAMS

        block = ctx.enter_context(nc.Block())

        @block.sync
        def _(sp):
            for dst, src in ((ident_sb[:, :], ident), (w_in_sb[:, :, :], w_in), (chan_sb[:, :, :, :], chan),
                             (w_x_sb[:, :, :, :], w_x), (w_delta_sb[DT_ROWS, :, :], w_delta), (a_sb[:, :], a_log), (sel_sb[:, :, :], sel), (minus_sb[:, :], minus),
                             (w_out_sb[:, :, :, :], w_out), (w_r_sb[:, :], w_r)):
                sp.dma_start(dst, src).then_inc(w_loaded, 16)
            for t in range(2):
                sp.dma_start(x_stage[:, t], x_t[t]).then_inc(x_loaded[t], 16)
            sp.dma_start(b_r_sb[:, :], b_r.rearrange("(a e) -> a e", a=1).to_broadcast([P, EXPERTS])).then_inc(bias_loaded, 16)
            sp.dma_start(residual[:, :, :], x.rearrange("s (b p) d -> p (s b) d", p=P)).then_inc(residual_loaded, 16)
            sp.wait_ge(zeroed, 1)
            sp.dma_start(sorted_x.ap().rearrange("(b p) d -> p b d", p=P),
                         zero_rows[:, :].unsqueeze(1).to_broadcast([P, sorted_blocks, D_MODEL])).then_inc(pad_zeroed, 16)
            with sp.Fori(1, tiles // 2) as j:
                for half in range(2):
                    transposed = sp.snap((j * 2 + (half - 2)) // STREAMS * ROUND + (j * 2 + (half - 2)) % STREAMS + 1)
                    sp.wait_ge(w_loaded, 16 * WEIGHT_DMAS)
                    sp.wait_ge(in_mm, transposed)
                    sp.dma_start(x_stage[:, half], x_t[bass.ds(j * 2 + half, 1)].rearrange("t p b d -> (t p) b d")
                                 ).then_inc(x_loaded[half], 16)

            sp.wait_ge(res_done, tiles)
            sp.dma_start(order_sb[:, 0:2 * P + blocks + sorted_blocks], order).then_inc(order_loaded, 16)
            sp.dma_start(w1_sb, w1).then_inc(experts_loaded, 16)
            sp.dma_start(w2_sb, w2).then_inc(experts_loaded, 16)

            def group_rows(dram, g):
                return dram[bass.ds(g, 1)].rearrange("g p b d -> (g p) b d")

            def load_group(g, i):
                sp.dma_start(sorted_in[i].rearrange("p (b d) -> p b d", b=GROUP), group_rows(sorted_x_g, g)
                             ).then_inc(sorted_loaded[i], 16)

            def store_group(g, i, count):
                sp.wait_ge(w_loaded, 16 * WEIGHT_DMAS)
                sp.wait_ge(y_copied, count)
                sp.dma_start(group_rows(sorted_y_g, g), y_stage[i].rearrange("p (b d) -> p b d", b=GROUP)
                             ).then_inc(y_stored[i], 16)

            sp.wait_ge(scattered, 16 * blocks)
            for i in range(2):
                load_group(i, i)
            with sp.Fori(0, groups // 2 - 1) as j:
                for i in range(2):
                    used = sp.snap(j * 2 + (i + 1))
                    sp.wait_ge(w_loaded, 16 * WEIGHT_DMAS)
                    sp.wait_ge(st_mm, used)
                    load_group(j * 2 + (i + 2), i)
                    store_group(j * 2 + i, i, used)
            for i in range(2):
                store_group(groups - 2 + i, i, groups - 1 + i)
            with sp.Fori(0, tiles // 2) as j:
                for half in range(2):
                    made = sp.snap(j * 2 + (half + 1))
                    sp.wait_ge(w_loaded, 16 * WEIGHT_DMAS)
                    sp.wait_ge(o_ready, made)
                    sp.dma_start(out_t[bass.ds(j * 2 + half, 1)].rearrange("t p b d -> (t p) b d"),
                                 out_stage[half].rearrange("p (b d) -> p b d", b=BLK)).then_inc(stored[half], 16)
            for half in range(2):
                sp.wait_ge(stored[half], 16 * (tiles // 2))

        @block.tensor
        def _(pe):
            def project_in(p, k):
                if isinstance(p, int) and p < STREAMS - 1:
                    wait(pe, in_ready, p)
                else:
                    pe.wait_ge(sp_abs, 4 * (p - 1))
                if layer_of(k) == 0:
                    pe.wait_ge(x_loaded[k % 2], round_of(p, k) * 32 + (k % STREAMS // 2 + 1) * 16)
                    for b in range(BLK):
                        last = pe.transpose(ps_j[:, b * P:(b + 1) * P], x_stage[:, k % 2, b, :], ident_sb[:, :])
                else:
                    pe.wait_ge(gate_ready, p - STREAMS + 1)
                    for h in range(HALVES):
                        last = pe.matmul(ps_j[:, :], w_out_sb[:, layer_of(k) - 1, h, :], gated[:, h, :],
                                         start=(h == 0), stop=(h == HALVES - 1))
                last.then_inc(in_mm, 1)

            def project_out(s):
                pe.wait_ge(gate_ready, s + 1)
                if is_last(s, STREAMS):
                    pe.wait_ge(sp_abs, 4 * min(s + 3, steps))
                else:
                    pe.wait_ge(in_ready, s + STREAMS + 1)
                for b in range(BLK):
                    for h in range(HALVES):
                        last = pe.matmul(ps_j[:, b * P:(b + 1) * P], gated[:, h, b * P:(b + 1) * P],
                                         w_out_sb[:, LAYERS - 1, h, :], start=(h == 0), stop=(h == HALVES - 1))
                last.then_inc(out_mm, 1)

            def half_in(k, which, done):
                pe.matmul(ps_j[:, :], w_in_sb[:, layer_of(k), which * P:(which + 1) * P], layer_in[:, k % STREAMS, :],
                          start=True, stop=True).then_inc(done, 1)

            def project_u(p, k, h):
                if h == 0:
                    pe.wait_ge(in_ready, min(max(p + 2, STREAMS - 1), steps) if isinstance(p, int) else p + 2)
                    if layer_of(k - 3) == LAYERS - 1 and not (isinstance(p, int) and p < 3):
                        pe.wait_ge(res_done, tile_of(p - 3, k - 3) + 1)
                    else:
                        wait(pe, sp_abs, 4 * p)
                else:
                    pe.wait_ge(u_taken, 2 * p + 1)
                half_in(k, h, u_mm)

            def project_z(p, k, h):
                if h == 0:
                    pe.wait_ge(u_taken, 2 * p + 2)
                else:
                    pe.wait_ge(z_taken, 2 * p + 1)
                half_in(k, HALVES + h, z_mm)

            def project_x(p, k):
                pe.wait_ge(u_ready, p + 1)
                pe.wait_ge(z_taken, 2 * p + 2)
                for h in range(HALVES):
                    last = pe.matmul(ps_j[:, :], w_x_sb[:, layer_of(k), h, :], u[:, k % 2, h, :],
                                     start=(h == 0), stop=(h == HALVES - 1))
                last.then_inc(x_mm, 1)

            def subtract_parts(p, k, i):
                if i == 0:
                    pe.wait_ge(bc_hi, p + 1)
                    pe.wait_ge(dt_ready, p + 1)
                else:
                    pe.wait_ge(bc_mid_s, p + 1)
                pe.matmul(ps_j[:, :], minus_sb[:, :], bc_parts[0:2 * BC, k % 2, :], start=False, stop=True,
                          skip_group_check=True).then_inc(rest_mm, 1)

            def project_delta(p, k, h):
                if h == 0:
                    pe.wait_ge(dt_ready, p + 1)
                    pe.wait_ge(bc_lo, p + 1)
                else:
                    pe.wait_ge(sp_abs, 4 * p + 2)
                pe.matmul(ps_j[:, :], w_delta_sb[DT_ROWS, layer_of(k), h * P:(h + 1) * P], dt_rows[DT_ROWS, :],
                          start=True, stop=True).then_inc(delta_mm, 1)

            def broadcast_b(s, k, n):
                q = s * D_STATE + n
                if n == 0:
                    pe.wait_ge(bc_lo, s + 1)
                wait(pe, dbu_ready, q - 1)
                pe.matmul(ps_b[n % 2][:, :], sel_sb[:, n, :], bc_parts[:, k % 2, :], start=True, stop=True).then_inc(b_ready, 1)

            def broadcast_c(s, k, n):
                wait(pe, c_copied, s * D_STATE + n)
                pe.matmul(ps_c[:, :], sel_sb[:, D_STATE + n, :], bc_parts[:, k % 2, :], start=True, stop=True).then_inc(c_ready, 1)

            def sum_states(s, n):
                q = s * D_STATE + n
                pe.wait_ge(ch_ready, q + 1)
                if n == 0:
                    wait(pe, y_taken, s)
                for h in range(HALVES):
                    last = pe.matmul(ps_y[h][:, :], ident_sb[:, :], ch[:, n % RING, h, :],
                                     start=(n == 0), stop=(n == D_STATE - 1))
                last.then_inc(y_mm, 1)

            def step(s, k):
                if is_step(s, 0):
                    broadcast_b(s, k, 0)
                for n in range(D_STATE):
                    if n + 1 < D_STATE:
                        broadcast_b(s, k, n + 1)
                    elif not is_last(s):
                        broadcast_b(s + 1, k + 1, 0)
                    if n < LAG and not is_step(s, 0):
                        sum_states(s - 1, D_STATE - LAG + n)
                    if n >= LAG:
                        sum_states(s, n - LAG)
                    broadcast_c(s, k, n)
                    if not is_last(s):
                        if n in (AT_U, AT_U + 1):
                            project_u(s + 1, k + 1, n - AT_U)
                        if n in (AT_Z, AT_Z + 1):
                            project_z(s + 1, k + 1, n - AT_Z)
                        if n == AT_X:
                            project_x(s + 1, k + 1)
                        if n == AT_REST:
                            subtract_parts(s + 1, k + 1, 0)
                        if n == AT_REST2:
                            subtract_parts(s + 1, k + 1, 1)
                        if n in (AT_DELTA, AT_DELTA + 1):
                            project_delta(s + 1, k + 1, n - AT_DELTA)
                    if n == AT_IN and not is_last(s, STREAMS - 1):
                        project_in(s + STREAMS - 1, k + STREAMS - 1)
                    if n == AT_OUT and layer_of(k - 1) == LAYERS - 1 and not is_step(s, 0):
                        project_out(s - 1)

            pe.wait_ge(w_loaded, 16 * WEIGHT_DMAS)
            for p in range(STREAMS - 1):
                project_in(p, p)
            for h in range(HALVES):
                project_u(0, 0, h)
            for h in range(HALVES):
                project_z(0, 0, h)
            project_x(0, 0)
            subtract_parts(0, 0, 0)
            subtract_parts(0, 0, 1)
            for h in range(HALVES):
                project_delta(0, 0, h)
            run_steps(pe, step)
            for n in range(D_STATE - LAG, D_STATE):
                sum_states(steps - 1, n)
            project_out(steps - 1)

            def transpose_x1(t, i):
                pe.wait_ge(x1_ready, t + 1)
                wait(pe, xt_ready, t - 1)
                for b in range(BLK):
                    last = pe.transpose(ps_b[i][:, b * P:(b + 1) * P],
                                        x1[:, t * BLK + b, :], ident_sb[:, :])
                last.then_inc(xt_mm, 1)

            def logits(t, i):
                pe.wait_ge(xt_ready, t + 1)
                for b in range(BLK):
                    last = pe.matmul(blocks_of(ps_c[:, :])[:, t * BLK + b, :], x1_t[i][:, b * P:(b + 1) * P],
                                     w_r_sb[:, :], start=True, stop=True)
                last.then_inc(lg_mm, 1)

            transpose_x1(0, 0)
            for t in range(1, tiles):
                transpose_x1(t, t % 2)
                logits(t - 1, 1 - t % 2)
            logits(tiles - 1, 1)

            pe.wait_ge(order_loaded, 16)
            pe.wait_ge(placed, COUNTED)
            counts = experts_of(cum)[:, :, blocks - 1]
            pe.matmul(ps_j[:, 0:EXPERTS], before, counts, start=True, stop=True)
            pe.matmul(ps_j[:, EXPERTS:2 * EXPERTS], ones, counts, start=True, stop=True).then_inc(count_mm, 1)

            def transpose_sorted(g, i, loads):
                pe.wait_ge(sorted_loaded[i], 16 * loads)
                wait(pe, st_ready, g - 1)
                for b in range(GROUP):
                    last = pe.transpose(ps_b[i][:, b * P:(b + 1) * P], sorted_in[i][:, b * P:(b + 1) * P], ident_sb[:, :])
                last.then_inc(st_mm, 1)

            def up(c, k, j):
                if k % GROUP == 0:
                    pe.wait_ge(st_ready, j * 2 + (k // GROUP + 1))
                pe.wait_ge(weights_ready, c + 1)
                wait(pe, gelu_s, c - 1)
                for f in range(FCH):
                    last = pe.matmul(hid_banks[k % 2][:, f * P:(f + 1) * P], weights[k % HAND_OVER][:, f * P:(f + 1) * P],
                                     sorted_t[k // GROUP][:, k % GROUP * P:(k % GROUP + 1) * P], start=True, stop=True)
                last.then_inc(up_mm, 1)

            def down(c, k, j):
                pe.wait_ge(gelu_s, c + 1)
                if k % GROUP == 0:
                    wait(pe, y_copied, j * 2 + (k // GROUP - 1))
                for f in range(FCH):
                    last = pe.matmul(y_banks[k // GROUP][:, k % GROUP * P:(k % GROUP + 1) * P], hid[k % 2][:, f * P:(f + 1) * P],
                                     weights[k % HAND_OVER][:, FFN + f * D_MODEL:FFN + (f + 1) * D_MODEL],
                                     start=(f == 0), stop=(f == FCH - 1))
                last.then_inc(down_mm, 1)

            def two_groups(c, j, last):
                for k in range(2 * GROUP):
                    if not (last and k == 2 * GROUP - 1):
                        up(c + (k + 1), (k + 1) % (2 * GROUP), j + (k + 1) // (2 * GROUP))
                    if k == 1:
                        transpose_sorted(j * 2 + 1, 1, j + 1)
                    if k == GROUP + 1 and not last:
                        transpose_sorted(j * 2 + 2, 0, j + 2)
                    down(c + k, k, j)

            transpose_sorted(0, 0, 1)
            up(0, 0, 0)
            two_groups(0, 0, False)
            with pe.Fori(1, groups // 2 - 1) as j:
                two_groups(j * (2 * GROUP), j, False)
            two_groups(sorted_blocks - 2 * GROUP, groups // 2 - 1, True)

        @block.scalar
        def _(act):
            CONV_B, DELTA_B, SKIP = D_CONV, D_CONV + 1, D_CONV + 2

            def chan_of(k, h, c):
                return chan_sb[:, layer_of(k), h, c:c + 1]

            def take_in(p, k):
                act.wait_ge(in_mm, p + 1)
                act.copy(layer_in[:, k % STREAMS, :], ps_j[:, :]).then_inc(in_ready, 1)

            def take_u(p, k, h):
                if h == 0:
                    wait(act, u_ready, p)
                act.wait_ge(u_mm, 2 * p + h + 1)
                act.activation(conv[:, h, :], ps_j[:, :], ACT.Identity, bias=chan_of(k, h, CONV_B),
                               scale=chan_of(k, h, D_CONV - 1)).then_inc(conv_init, 1)
                act.copy(u_raw[:, h, :], ps_j[:, :]).then_inc(u_taken, 1)

            def take_z(p, h):
                if h == 0:
                    wait(act, delta_ready, p)
                act.wait_ge(z_mm, 2 * p + h + 1)
                act.copy(z_raw[:, h, :], ps_j[:, :]).then_inc(z_taken, 1)

            def silu_u(p, k):
                act.wait_ge(conv_done, 2 * p + 2)
                wait(act, y_taken, p - 1)
                act.activation(u[:, k % 2], conv[:, :, :], ACT.Silu).then_inc(u_ready, 1)

            def silu_z(p, k):
                wait(act, gate_ready, p - 1)
                act.wait_ge(z_taken, 2 * p + 2)
                act.activation(z_gate[:, k % 2], z_raw[:, :, :], ACT.Silu).then_inc(z_ready, 1)
                act.preload_act_table_set("natural_log_exp_and_others")

            def split_high(p, k):
                act.wait_ge(x_mm, p + 1)
                act.copy(bc_parts[0:2 * BC, k % 2, :], ps_j[0:2 * BC, :]).then_inc(bc_hi, 1)

            def take_dt(p, k):
                act.wait_ge(x_mm, p + 1)
                act.copy(dt_rows[DT_ROWS, :], ps_j[DT_ROWS, :]).then_inc(dt_ready, 1)

            def split_mid(p, k):
                act.wait_ge(rest_mm, 2 * p + 1)
                act.copy(bc_parts[BC:2 * BC, k % 2, :], ps_j[BC:2 * BC, :]).then_inc(bc_mid_s, 1)

            def split_low(p, k):
                act.wait_ge(rest_mm, 2 * p + 2)
                act.copy(bc_parts[2 * BC:3 * BC, k % 2, :], ps_j[BC:2 * BC, :]).then_inc(bc_lo, 1)

            def softplus_parts(p, k, h):
                if h == 0:
                    wait(act, delta_ready, p)
                    act.wait_ge(z_ready, p + 1)
                act.wait_ge(delta_mm, 2 * p + h + 1)
                bias = chan_of(k, h, DELTA_B)
                act.activation(sp_exp[:, h, :], ps_j[:, :], ACT.Abs, bias=bias).then_inc(sp_abs, 1)
                act.activation(sp_relu[:, h, :], ps_j[:, :], ACT.Relu, bias=bias).then_inc(sp_abs, 1)

            def softplus_exp(p):
                act.wait_ge(sp_abs, 4 * (p + 1))
                act.activation(sp_exp[:, :, :], sp_exp[:, :, :], ACT.Exp, scale=-1.0).then_inc(sp_e, 1)

            def softplus_ln(p):
                act.wait_ge(sp_e, p + 1)
                act.activation(sp_exp[:, :, :], sp_exp[:, :, :], ACT.Ln, bias=1.0).then_inc(sp_ln, 1)

            def copy_c(s, n):
                q = s * D_STATE + n
                wait(act, ch_ready, q - RING + 1)
                act.wait_ge(c_ready, q + 1)
                act.copy(c_bcast[:, n % RING, :], ps_c[:, :]).then_inc(c_copied, 1)

            def decay(s, k, n):
                if n == 0:
                    act.wait_ge(delta_ready, s + 1)
                for h in range(HALVES):
                    wait(act, scanned, 2 * (s * D_STATE + last_user(n)) + h + 1)
                    col = (layer_of(k) * HALVES + h) * D_STATE + n
                    act.activation(decay_buffer(n, h).rearrange("p (s t) -> p s t", s=SPT)[:, :, 1:SEQ],
                                   delta[:, k % 2, h, :].rearrange("p (s t) -> p s t", s=SPT)[:, :, 1:SEQ],
                                   ACT.Exp, scale=a_sb[:, col:col + 1]).then_inc(da_ready, 1)

            def step(s, k):
                made = 0
                for n in range(D_STATE):
                    while made <= n or (n in DECAYS_BY and made <= DECAYS_BY[n]):
                        decay(s, k, made)
                        made += 1
                    copy_c(s, n)
                    if not is_last(s):
                        if n in (AT_U, AT_U + 1):
                            take_u(s + 1, k + 1, n - AT_U)
                        if n in (AT_Z, AT_Z + 1):
                            take_z(s + 1, n - AT_Z)
                        if n == AT_SILU:
                            silu_u(s + 1, k + 1)
                        if n == AT_SILU_Z:
                            silu_z(s + 1, k + 1)
                        if n == AT_HIGH:
                            split_high(s + 1, k + 1)
                            take_dt(s + 1, k + 1)
                        if n == AT_MID:
                            split_mid(s + 1, k + 1)
                        if n == AT_LOW:
                            split_low(s + 1, k + 1)
                        if n in (AT_DELTA, AT_DELTA + 1):
                            softplus_parts(s + 1, k + 1, n - AT_DELTA)
                        if n == AT_EXP:
                            softplus_exp(s + 1)
                        if n == AT_LN:
                            softplus_ln(s + 1)
                    if n == AT_TAKE_IN and not is_last(s, STREAMS - 1):
                        take_in(s + STREAMS - 1, k + STREAMS - 1)

            act.wait_ge(w_loaded, 16 * WEIGHT_DMAS)
            act.activation(a_exp[:, :], a_sb[:, :], ACT.Exp).then_inc(a_neg, 1)
            act.wait_ge(a_neg, 1)
            act.mul(a_sb[:, :], a_exp[:, :], -1.0).then_inc(a_ready, 1)
            for p in range(STREAMS - 1):
                take_in(p, p)
            for h in range(HALVES):
                take_u(0, 0, h)
            for h in range(HALVES):
                take_z(0, h)
            silu_u(0, 0)
            silu_z(0, 0)
            split_high(0, 0)
            take_dt(0, 0)
            split_mid(0, 0)
            split_low(0, 0)
            for h in range(HALVES):
                softplus_parts(0, 0, h)
            softplus_exp(0)
            softplus_ln(0)
            act.wait_ge(a_ready, 1)
            act.wait_ge(zeroed, 4)
            run_steps(act, step)

            def take_x1_t(t, i):
                act.wait_ge(xt_mm, t + 1)
                wait(act, lg_mm, t - 1)
                act.copy(x1_t[i], ps_b[i][:, :]).then_inc(xt_ready, 1)

            take_x1_t(0, 0)
            take_x1_t(1, 1)
            with act.Fori(1, tiles // 2) as j:
                for i in range(2):
                    take_x1_t(j * 2 + i, i)
            act.wait_ge(routed, MAX_FOUND)
            act.activation(prob_t, lg_max, ACT.Tanh, scale=0.5).then_inc(tanh_s, 1)

            def take_sorted_t(g, i):
                act.wait_ge(st_mm, g + 1)
                wait(act, up_mm, (g - 1) * GROUP)
                act.copy(sorted_t[i], ps_b[i][:, :]).then_inc(st_ready, 1)

            def gelu(c, k):
                act.wait_ge(up_mm, c + 1)
                wait(act, down_mm, c - 1)
                act.activation(hid[k % 2], hid_banks[k % 2][:, :], ACT.Gelu).then_inc(gelu_s, 1)

            def take_y(g, i, stores):
                act.wait_ge(down_mm, (g + 1) * GROUP)
                wait(act, y_stored[i], 16 * stores)
                act.copy(y_stage[i], y_banks[i][:, :]).then_inc(y_copied, 1)

            def two_groups(c, j, first, last):
                for k in range(2 * GROUP):
                    gelu(c + k, k)
                    if k == 0 and not first:
                        take_y(j * 2 - 1, 1, j - 1)
                    if k == GROUP:
                        take_y(j * 2, 0, j)
                    if k == 2:
                        take_sorted_t(j * 2 + 1, 1)
                    if k == GROUP + 2 and not last:
                        take_sorted_t(j * 2 + 2, 0)

            take_sorted_t(0, 0)
            two_groups(0, 0, True, False)
            two_groups(2 * GROUP, 1, False, False)
            with act.Fori(2, groups // 2 - 1) as j:
                two_groups(j * (2 * GROUP), j, False, False)
            two_groups(sorted_blocks - 2 * GROUP, groups // 2 - 1, False, True)
            take_y(groups - 1, 1, groups // 2 - 1)

        @block.vector
        def _(dve):
            SKIP = D_CONV + 2

            def conv_taps(p, k, shift, h):
                src = u_raw[:, h, :].rearrange("p (s t) -> p s t", s=SPT)[:, :, 0:SEQ - shift]
                acc = conv[:, h, :].rearrange("p (s t) -> p s t", s=SPT)[:, :, shift:SEQ]
                if shift == 1:
                    dve.wait_ge(u_taken, 2 * p + h + 1)
                else:
                    dve.wait_ge(conv_tap, 4 * p + 2 * (shift - 2) + h + 1)
                tap = dve.scalar_tensor_tensor(acc, src, chan_sb[:, layer_of(k), h, D_CONV - 1 - shift:D_CONV - shift], acc,
                                               ALU.mult, ALU.add)
                if shift < D_CONV - 1:
                    tap.then_inc(conv_tap, 1)
                else:
                    tap.then_inc(conv_done, 1)

            def make_delta(p, k):
                dve.wait_ge(sp_ln, p + 1)
                dve.tensor_tensor(delta[:, k % 2], sp_relu[:, :, :], sp_exp[:, :, :], ALU.add).then_inc(delta_ready, 1)

            def take_y(s, k):
                dve.wait_ge(y_mm, (s + 1) * D_STATE)
                if not is_step(s, 0):
                    if layer_of(k - 1) == LAYERS - 1:
                        dve.wait_ge(out_mm, tile_of(s - 1, k - 1) + 1)
                    else:
                        dve.wait_ge(in_mm, s + STREAMS)
                for h in range(HALVES):
                    last = dve.scalar_tensor_tensor(y_skip[:, h, :], u[:, k % 2, h, :], chan_sb[:, layer_of(k), h, SKIP:SKIP + 1],
                                                    ps_y[h][:, :], ALU.mult, ALU.add)
                last.then_inc(y_taken, 1)

            def add_residual(s, k):
                t = tile_of(s, k)
                dve.wait_ge(out_mm, t + 1)
                dve.wait_ge(residual_loaded, 16)
                rows = residual[:, bass.ds(t * BLK, BLK), :]
                dve.tensor_tensor(rows, ps_j[:, :].rearrange("p (b d) -> p b d", b=BLK), rows, ALU.add).then_inc(res_done, 1)

            def inputs(s, k, n):
                q = s * D_STATE + n
                if n == 0:
                    dve.wait_ge(du_ready, s + 1)
                dve.wait_ge(b_ready, q + 1)
                wait(dve, scanned, 2 * (q - RING + 1))
                dve.tensor_tensor(dbu[:, n % RING, :].rearrange("p (h t) -> p h t", h=HALVES), du[:, k % 2],
                                  ps_b[n % 2][:, :].unsqueeze(1).to_broadcast([P, HALVES, T]), ALU.mult).then_inc(dbu_ready, 1)

            def scan(s, n):
                q = s * D_STATE + n
                dve.wait_ge(dbu_ready, q + 1)
                wait(dve, ch_ready, q - RING + 1)
                for h in range(HALVES):
                    dve.wait_ge(da_ready, 2 * q + h + 1)
                    dve.tensor_tensor_scan(h_state[:, n % RING, h * T:(h + 1) * T], decay_buffer(n, h),
                                           dbu[:, n % RING, h * T:(h + 1) * T], 0.0, ALU.mult, ALU.add).then_inc(scanned, 1)

            CONV_AT = {2: ((1, 0),), 3: ((1, 1), (2, 0), (2, 1)), 4: ((3, 0), (3, 1))}

            def step(s, k):
                if is_step(s, 0):
                    inputs(s, k, 0)
                for n in range(D_STATE):
                    if n + 1 < D_STATE:
                        inputs(s, k, n + 1)
                    scan(s, n)
                    if n == AT_Y and not is_step(s, 0):
                        take_y(s - 1, k - 1)
                    if not is_last(s):
                        for shift, h in CONV_AT.get(n, ()):
                            conv_taps(s + 1, k + 1, shift, h)
                    if n == AT_SUM and not is_last(s):
                        make_delta(s + 1, k + 1)
                    if n == AT_RESIDUAL and layer_of(k - 1) == LAYERS - 1 and not is_step(s, 0):
                        add_residual(s - 1, k - 1)
                if not is_last(s):
                    inputs(s + 1, k + 1, 0)

            dve.memset(zero_rows[:, :], 0.0).then_inc(zeroed, 1)
            dve.memset(decays[:, :, :], 0.0).then_inc(zeroed, 1)
            dve.memset(ps_da0[:, :], 0.0).then_inc(zeroed, 1)
            dve.memset(ps_da1[:, :], 0.0).then_inc(zeroed, 1)
            dve.wait_ge(w_loaded, 16 * WEIGHT_DMAS)
            for shift in (1, 2, 3):
                for h in range(HALVES):
                    conv_taps(0, 0, shift, h)
            make_delta(0, 0)
            run_steps(dve, step)
            take_y(steps - 1, ROUND - 1)
            add_residual(steps - 1, ROUND - 1)

            dve.wait_ge(res_done, tiles)

            def rows(t, b):
                return x1[:, bass.ds(t * BLK + b, 1), :].rearrange("p a d -> p (a d)")

            for part in range(PARTS_OF_NORM):
                of_part = range(part * blocks // PARTS_OF_NORM, (part + 1) * blocks // PARTS_OF_NORM)
                for b in of_part:
                    last = dve.bn_stats(ln_stats[:, b, :], x1[:, b, :])
                last.then_inc(stats, 1)
                dve.wait_ge(stats, part + 1)
                dve.memset(scratch[:, :], 0.0)
                for b in of_part:
                    last = dve.bn_aggr(ln_mv[:, b, :], ln_stats[:, b, :])
                last.then_inc(mv, 1)
            for e in range(EXPERTS):
                dve.memset(blocks_of(prio)[:, :, e:e + 1], float(EXPERTS - e))
            dve.memset(ones_e, 1.0)
            dve.memset(keep, 1.0).then_inc(consts_set, 1)
            dve.wait_ge(consts_set, 1)
            dve.memset(experts_of(keep)[:, :, 0:1], 0.0).then_inc(consts_set, 1)
            for part in range(PARTS_OF_NORM):
                dve.wait_ge(rstd_s, part + 1)
                with dve.Fori(part * tiles // PARTS_OF_NORM, (part + 1) * tiles // PARTS_OF_NORM) as t:
                    tile_rows = x1[:, bass.ds(t * BLK, BLK), :]
                    dve.tensor_tensor(tile_rows, tile_rows,
                                      ln_mv[:, bass.ds(t * BLK, BLK), 0:1].to_broadcast([P, BLK, D_MODEL]),
                                      ALU.subtract).then_inc(centred, 1)
                    dve.wait_ge(centred, t + 1)
                    dve.tensor_tensor(tile_rows, tile_rows,
                                      ln_rstd[:, bass.ds(t * BLK, BLK)].unsqueeze(2).to_broadcast([P, BLK, D_MODEL]),
                                      ALU.mult).then_inc(x1_ready, 1)

            dve.wait_ge(lg_mm, tiles)
            dve.wait_ge(bias_loaded, 16)
            dve.tensor_tensor(blocks_of(lg), blocks_of(ps_c[:, :]), b_r_sb[:, :].unsqueeze(1).to_broadcast([P, blocks, EXPERTS]),
                              ALU.add).then_inc(routed, 1)
            dve.wait_ge(routed, 1)
            dve.tensor_scalar(lg, lg, SIGMOID_ONE, None, ALU.min).then_inc(routed, 1)
            dve.wait_ge(routed, 2)
            dve.tensor_reduce(lg_max, blocks_of(lg), AX_X, ALU.max).then_inc(routed, 1)
            dve.wait_ge(routed, MAX_FOUND)
            dve.tensor_tensor(blocks_of(rank), blocks_of(lg), lg_max.unsqueeze(2).to_broadcast([P, blocks, EXPERTS]),
                              ALU.is_equal).then_inc(routed, 1)
            dve.wait_ge(routed, 4)
            dve.wait_ge(consts_set, 2)
            dve.tensor_tensor(rank, rank, prio, ALU.mult).then_inc(routed, 1)
            dve.wait_ge(routed, 5)
            dve.tensor_reduce(pos[:, :], blocks_of(rank), AX_X, ALU.max).then_inc(routed, 1)
            dve.wait_ge(routed, 6)
            dve.tensor_tensor(experts_of(mask), blocks_of(rank).rearrange("p b e -> p e b"),
                              pos[:, :].unsqueeze(1).to_broadcast([P, EXPERTS, blocks]), ALU.is_equal).then_inc(routed, 1)
            dve.wait_ge(routed, 7)

            dve.tensor_tensor_scan(cum, keep, mask, 0.0, ALU.mult, ALU.add).then_inc(placed, 1)
            dve.wait_ge(count_mm, 1)
            dve.tensor_copy(total, ps_j[:, EXPERTS:2 * EXPERTS]).then_inc(placed, 1)
            dve.wait_ge(placed, 2)
            dve.tensor_tensor(experts_of(at_pos), total.unsqueeze(2).to_broadcast([P, EXPERTS, blocks]),
                              fills.unsqueeze(1).to_broadcast([P, EXPERTS, blocks]), ALU.is_gt).then_inc(placed, 1)
            dve.wait_ge(placed, 3)
            dve.tensor_reduce(padded, experts_of(at_pos), AX_X, ALU.add).then_inc(placed, 1)
            dve.wait_ge(placed, 4)
            dve.tensor_tensor_scan(end, ones_e, padded, 0.0, ALU.mult, ALU.add).then_inc(placed, 1)
            dve.wait_ge(placed, 5)
            dve.tensor_tensor(base, end, padded, ALU.subtract).then_inc(placed, 1)
            dve.wait_ge(placed, 6)
            dve.scalar_tensor_tensor(base, base, float(P), ps_j[:, 0:EXPERTS], ALU.mult, ALU.add).then_inc(placed, 1)
            dve.wait_ge(placed, 7)
            dve.tensor_tensor(experts_of(at_pos), experts_of(cum), base.unsqueeze(2).to_broadcast([P, EXPERTS, blocks]),
                              ALU.add).then_inc(placed, 1)
            dve.wait_ge(placed, 8)
            dve.tensor_tensor(at_pos, at_pos, mask, ALU.mult).then_inc(placed, 1)
            dve.wait_ge(placed, 9)
            dve.tensor_reduce(pos[:, :], experts_of(at_pos).rearrange("p e b -> p b e"), AX_X, ALU.add).then_inc(placed, 1)
            dve.wait_ge(placed, 10)
            dve.tensor_scalar(row_of[:, :], pos[:, :], -1.0, None, ALU.add).then_inc(row_ready, 1)
            dve.tensor_tensor(ended.rearrange("p (j e) -> p j e", e=EXPERTS),
                              numbers.unsqueeze(2).to_broadcast([P, sorted_blocks, EXPERTS]),
                              end.unsqueeze(1).to_broadcast([P, sorted_blocks, EXPERTS]), ALU.is_ge).then_inc(placed, 1)
            dve.wait_ge(placed, 11)
            dve.tensor_reduce(ended_n[:, :], ended.rearrange("p (j e) -> p j e", e=EXPERTS), AX_X, ALU.add).then_inc(placed, 1)
            dve.wait_ge(placed, 12)
            dve.tensor_scalar(expert_of[:, :], ended_n[:, :], float(EXPERTS - 1), None, ALU.min).then_inc(expert_ready, 1)
            dve.wait_ge(tanh_s, 1)
            dve.tensor_scalar(prob[:, :], prob_t, 0.5, 0.5, ALU.mult, ALU.add).then_inc(prob_ready, 1)

            dve.wait_ge(expert_ready, 1)
            dve.wait_ge(experts_loaded, 16 * 2)

            def bring_weights(c, i):
                e = dve.value_load(expert_of[0:1, bass.ds(c, 1)], min_val=0, max_val=EXPERTS - 1)
                wait(dve, down_mm, c - (HAND_OVER - 1))
                dve.tensor_scalar(weights[i][:, 0:FFN], w1_sb[:, bass.ds(e, 1), :].rearrange("p a f -> p (a f)"),
                                  1.0, None, ALU.mult)
                dve.tensor_scalar(weights[i][:, FFN:2 * FFN], w2_sb[:, bass.ds(e, 1), :].rearrange("p a f -> p (a f)"),
                                  1.0, None, ALU.mult).then_inc(weights_ready, 1)

            for i in range(HAND_OVER):
                bring_weights(i, i)
            with dve.Fori(1, sorted_blocks // HAND_OVER) as j:
                for i in range(HAND_OVER):
                    bring_weights(j * HAND_OVER + i, i)

            def second_stats(t, i, rounds):
                dve.wait_ge(gathered[i], 16 * BLK * rounds)
                for b in range(BLK):
                    cols = slice(b * P, (b + 1) * P)
                    last = dve.scalar_tensor_tensor(x2[i][:, cols], y_back[i][:, cols], prob[:, bass.ds(t * BLK + b, 1)],
                                                    rows(t, b), ALU.mult, ALU.add)
                last.then_inc(x2_ready, 1)
                dve.wait_ge(x2_ready, t + 1)
                for b in range(BLK):
                    last = dve.bn_stats(ln_stats2[:, i, b, :], x2[i][:, b * P:(b + 1) * P])
                last.then_inc(stats2, 1)
                dve.wait_ge(stats2, t + 1)
                dve.memset(scratch[:, :], 0.0)
                for b in range(BLK):
                    last = dve.bn_aggr(ln_mv2[:, i, b, :], ln_stats2[:, i, b, :])
                last.then_inc(mv2, 1)

            def finish(t, i):
                dve.wait_ge(rstd2_s, t + 1)
                wait(dve, stored[i % 2], 8 * (t - i % 2))
                for b in range(BLK):
                    cols = slice(b * P, (b + 1) * P)
                    last = dve.tensor_scalar(out_stage[i % 2][:, cols], x2[i][:, cols], ln_mv2[:, i, b, 0:1],
                                             ln_rstd2[:, i, b:b + 1], ALU.subtract, ALU.mult)
                last.then_inc(o_ready, 1)

            def round_of_tiles(t, rounds, first):
                for i in range(HAND_OVER):
                    second_stats(t + i, i, rounds)
                    if not (first and i < BEHIND):
                        finish(t + (i - BEHIND), (i - BEHIND) % HAND_OVER)

            dve.wait_ge(prob_ready, 1)
            round_of_tiles(0, 1, True)
            with dve.Fori(1, tiles // HAND_OVER) as j:
                round_of_tiles(j * HAND_OVER, j + 1, False)
            for t in range(tiles - BEHIND, tiles):
                finish(t, t % HAND_OVER)

        @block.gpsimd
        def _(pool):
            def make_du(p, k):
                pool.wait_ge(delta_ready, p + 1)
                pool.wait_ge(u_ready, p + 1)
                pool.tensor_tensor(du[:, k % 2], delta[:, k % 2], u[:, k % 2], ALU.mult).then_inc(du_ready, 1)

            def gate(s, k):
                pool.wait_ge(y_taken, s + 1)
                pool.wait_ge(z_ready, s + 1)
                pool.tensor_tensor(gated[:, :, :], y_skip[:, :, :], z_gate[:, k % 2], ALU.mult).then_inc(gate_ready, 1)

            def weigh(s, n):
                q = s * D_STATE + n
                pool.wait_ge(scanned, 2 * (q + 1))
                pool.wait_ge(c_copied, q + 1)
                wait(pool, y_mm, q - RING + 1)
                pool.tensor_tensor(ch[:, n % RING], h_state[:, n % RING, :].rearrange("p (h t) -> p h t", h=HALVES),
                                   c_bcast[:, n % RING, :].unsqueeze(1).to_broadcast([P, HALVES, T]), ALU.mult
                                   ).then_inc(ch_ready, 1)

            def step(s, k):
                for n in range(D_STATE):
                    weigh(s, n)
                    if n == AT_Y and not is_step(s, 0):
                        gate(s - 1, k - 1)
                    if n == AT_DU and not is_last(s):
                        make_du(s + 1, k + 1)

            make_du(0, 0)
            run_steps(pool, step)
            gate(steps - 1, ROUND - 1)

            pool.wait_ge(res_done, tiles)
            pool.memset(minus_half, -0.5)
            pool.memset(eps, EPS).then_inc(var_s, 1)
            pool.wait_ge(var_s, 1)
            for part in range(PARTS_OF_NORM):
                of_part = slice(part * blocks // PARTS_OF_NORM, (part + 1) * blocks // PARTS_OF_NORM)
                pool.wait_ge(mv, part + 1)
                pool.tensor_tensor(var_eps[:, of_part], ln_mv[:, of_part, 1], eps[:, of_part], ALU.add).then_inc(var_s, 1)
                pool.wait_ge(var_s, part + 2)
                pool.tensor_tensor(ln_rstd[:, of_part], var_eps[:, of_part], minus_half[:, of_part], ALU.pow
                                   ).then_inc(rstd_s, 1)

            pool.wait_ge(pad_zeroed, 16)
            pool.wait_ge(x1_ready, tiles)
            pool.wait_ge(row_ready, 1)
            for b in range(blocks):
                pool.indirect_dma_start(sorted_x[:, :], bass.IndirectOffsetOnAxis(ap=row_of[:, b:b + 1], axis=0),
                                        x1[:, b, :], None).then_inc(scattered, 16)

            def rstd2(t):
                i = t % HAND_OVER
                pool.wait_ge(mv2, t + 1)
                pool.tensor_tensor(var_eps2[:, i, :], ln_mv2[:, i, :, 1], eps[:, 0:BLK], ALU.add).then_inc(var2_s, 1)
                pool.wait_ge(var2_s, t + 1)
                if t >= HAND_OVER:
                    pool.wait_ge(o_ready, t - HAND_OVER + 1)
                pool.tensor_tensor(ln_rstd2[:, i, :], var_eps2[:, i, :], minus_half[:, 0:BLK], ALU.pow).then_inc(rstd2_s, 1)

            for i in range(2):
                pool.wait_ge(y_stored[i], 16 * (groups // 2))
            for t in range(tiles):
                i = t % HAND_OVER
                if t >= HAND_OVER:
                    pool.wait_ge(x2_ready, t - HAND_OVER + 1)
                for b in range(BLK):
                    pool.indirect_dma_start(y_back[i][:, b * P:(b + 1) * P], None, sorted_y[:, :],
                                            bass.IndirectOffsetOnAxis(ap=row_of[:, t * BLK + b:t * BLK + b + 1], axis=0)
                                            ).then_inc(gathered[i], 16)
                if t >= BEHIND:
                    rstd2(t - BEHIND)
            for t in range(tiles - BEHIND, tiles):
                rstd2(t)


def build(nc, args):
    layer_stack_moe(nc, *args)


def kernel(**inputs):
    import concourse.bacc as _bacc
    from concourse import mybir as _mybir
    from concourse.bass_utils import run_bass_kernel_spmd as _run

    a = {k.replace("L0_attn_", "").replace("L0_ffn_", ""): np.asarray(v) for k, v in inputs.items()}

    def by_channel(v):
        return v.reshape(LAYERS, HALVES, P, -1).transpose(2, 0, 1, 3)

    blocks = a["x"].shape[0] * a["x"].shape[1] // P
    sorted_blocks = sorted_blocks_of(blocks)
    xp = a["x_proj_w"].transpose(0, 2, 1).reshape(LAYERS, HALVES, P, -1).transpose(2, 0, 1, 3)
    arrays = {
        "x": a["x"],
        "w_in": a["in_proj_w"].transpose(2, 0, 1),
        "w_x": np.concatenate([xp[..., DT_RANK:], xp[..., DT_RANK:], xp[..., :DT_RANK]], axis=-1),
        "w_delta": a["dt_proj_w"].transpose(2, 0, 1),
        "w_out": a["out_proj_w"].transpose(0, 2, 1).reshape(LAYERS, HALVES, P, D_MODEL).transpose(2, 0, 1, 3),
        "chan": np.concatenate([by_channel(a["conv_w"]), by_channel(a["conv_b"]), by_channel(a["dt_proj_b"]),
                                by_channel(a["D"])], axis=-1),
        "a_log": by_channel(a["A_log"]).reshape(P, -1),
        "sel": np.tile(np.eye(BC, dtype=np.float32), (PARTS, 1))[:, :, None].repeat(P, 2).astype(_mybir.dt.np(BF16)),
        "minus": np.where(np.arange(P) < BC, 0.0, -np.eye(2 * BC, P)).astype(_mybir.dt.np(BF16)),
        "ident": np.eye(P, dtype=np.float32),
        "w_r": a["Wr"],
        "b_r": a["br"],
        "order": np.concatenate([np.triu(np.ones((P, P)), 1), np.ones((P, P)),
                                 np.tile(np.arange(blocks) * P, (P, 1)), np.tile(np.arange(sorted_blocks), (P, 1))],
                                axis=1).astype(np.float32),
        "w1": a["W1"].transpose(1, 0, 2),
        "w2": a["W2"].reshape(EXPERTS, FCH, P, D_MODEL).transpose(2, 0, 1, 3).reshape(P, EXPERTS, FFN),
    }
    nc = _bacc.Bacc("TRN2", target_bir_lowering=False, num_devices=1)
    feed, args = {}, []
    for name, v in arrays.items():
        v = np.ascontiguousarray(v)
        feed[f"in_{name}"] = v
        args.append(nc.dram_tensor(f"in_{name}", v.shape, _mybir.dt.from_np(v.dtype), kind="ExternalInput").ap())
    args.append(nc.dram_tensor("out", a["x"].shape, F32, kind="ExternalOutput").ap())
    build(nc, args)
    r = _run(nc, [feed], core_ids=[0])
    return r.results[0]["out"]
```
